# Optimizing a Trainium2 kernel written in Bass

```python
import numpy as np
import jax
import jax.numpy as jnp

def _softmax(x, axis=-1):
    return jax.nn.softmax(x, axis=axis)

def _gelu(x):
    return jax.nn.gelu(x, approximate=True)

def _silu(x):
    return jax.nn.silu(x)

def _sigmoid(x):
    return jax.nn.sigmoid(x)

def _layernorm(x, axis=-1, eps=1e-05):
    m = jnp.mean(x, axis=axis, keepdims=True)
    v = jnp.var(x, axis=axis, keepdims=True)
    return (x - m) / jnp.sqrt(v + eps)

def _scatter_add(tgt, idx, src, axis=0):
    return tgt.at[idx].add(src)

def _segment_sum(src, seg, n):
    return jax.ops.segment_sum(src, seg, n)
kernel_name = 'mk_sandwich_d1_jaxref_r8_d47453'

def setup_inputs(seed: int=0):
    np.random.seed(seed)
    _w = jnp.asarray

    def _L0_attn_setup():
        import jax, jax.numpy as jnp
        import numpy as np
        B, T, D_IN = (8, 512, 256)
        D_HIDDEN = 256
        D_OUT = 256
        N_BLOCKS = 8
        R_MIN, R_MAX = (0.9, 0.999)
        INIT_IMAG = 0.1

        def _lecun(key, shape, fan_in):
            return (jax.random.normal(key, shape, dtype=jnp.float32) * np.sqrt(1.0 / fan_in)).astype(jnp.float32)

        def _block_diag_linear(x, W, b):
            h, i, j = W.shape
            xb = x.reshape(x.shape[0], x.shape[1], h, i)
            y = jnp.einsum('bthi,hij->bthj', xb, W) + b
            return y.reshape(y.shape[0], y.shape[1], h * j)

        def _linear_scan(a, x):

            def combine(l, r):
                al, bl = l
                ar, br = r
                return (al * ar, ar * bl + br)
            _, h = jax.lax.associative_scan(combine, (a, x), axis=1)
            return h

        def _reference_tuple_inner(x, W_in, b_in, W_gx, b_gx, W_ga, b_ga, a_real, a_imag, W_out, b_out):
            xh = x @ W_in + b_in
            gate_x = jax.nn.sigmoid(_block_diag_linear(xh, W_gx, b_gx))
            gate_a = jax.nn.sigmoid(_block_diag_linear(xh, W_ga, b_ga))
            log_a_re = -8.0 * gate_a * jax.nn.softplus(a_real)
            log_a_im = a_imag * gate_a
            a = jnp.exp(jax.lax.complex(log_a_re, log_a_im))
            a_sq = jnp.exp(jax.lax.complex(2.0 * log_a_re, 2.0 * log_a_im))
            xr, xi = jnp.split(xh, 2, axis=-1)
            xc = jax.lax.complex(xr, xi) * gate_x
            xc = jnp.sqrt(1.0 - a_sq) * xc
            h = _linear_scan(a, xc)
            h_m = jnp.concatenate([h.real, h.imag], axis=-1)
            out = h_m @ W_out + b_out
            h_last = h_m[:, -1]
            return (out, h_last)
        key = jax.random.key(seed)
        ks = jax.random.split(key, 12)
        dh2 = D_HIDDEN // 2
        bin_, bout = (dh2 // N_BLOCKS, None)
        blk_in = D_HIDDEN // N_BLOCKS
        blk_out = dh2 // N_BLOCKS
        u1 = jax.random.uniform(ks[8], (dh2,))
        a_r = 0.5 * jnp.log(u1 * (R_MAX ** 2 - R_MIN ** 2) + R_MIN ** 2 + 1e-08)
        a_real = jnp.log(jnp.exp(-a_r) - 1.0)
        u2 = jax.random.uniform(ks[9], (dh2,))
        a_imag = jnp.pi * INIT_IMAG * u2
        return {'x': jax.random.normal(ks[0], (B, T, D_IN), dtype=jnp.float32), 'W_in': _lecun(ks[1], (D_IN, D_HIDDEN), D_IN), 'b_in': jnp.zeros((D_HIDDEN,), jnp.float32), 'W_gx': _lecun(ks[2], (N_BLOCKS, blk_in, blk_out), blk_in), 'b_gx': _lecun(ks[3], (N_BLOCKS, blk_out), blk_in), 'W_ga': _lecun(ks[4], (N_BLOCKS, blk_in, blk_out), blk_in), 'b_ga': _lecun(ks[5], (N_BLOCKS, blk_out), blk_in), 'a_real': a_real, 'a_imag': a_imag, 'W_out': _lecun(ks[6], (D_HIDDEN, D_OUT), D_HIDDEN), 'b_out': jnp.zeros((D_OUT,), jnp.float32)}
    _L0_attn_in = _L0_attn_setup()

    def _L0_ffn_setup():
        import jax, jax.numpy as jnp
        import numpy as np
        B, S, H, I, E, F, K, R, TOPK = (1, 128, 256, 176, 64, 8, 8, 8, 6)
        ISH = 2 * I

        def _fused_linear(x, W, qa, qb, scale, w):
            out = x @ W.T
            a = jnp.einsum('th,krh->tkr', x, qa)
            b = jnp.einsum('tkr,khr->tkh', a, qb)
            mix = jnp.einsum('tkh,tk->th', b, w)
            return out + scale[None, :] * mix

        def _moe_forward(hidden_states, gate_weight, inv_mapping, mask_up_W, gate_W, gate_qa, gate_qb, gate_scale, up_W, up_qa, up_qb, up_scale, down_W, down_qa, down_qb, down_scale, sh_gate_W, sh_up_W, sh_down_W):
            b, s, h = hidden_states.shape
            x = hidden_states.reshape(-1, h)
            T = x.shape[0]
            scores = jax.nn.softmax(x @ gate_weight.T, axis=-1)
            topk_w, topk_idx = jax.lax.top_k(scores, TOPK)
            w_dense = jnp.zeros((T, E), x.dtype).at[jnp.arange(T)[:, None], topk_idx].add(topk_w)
            flat = w_dense[:, inv_mapping]
            scalar = flat.sum(-1)
            soft = jax.nn.softmax(jnp.where(flat == 0, -1000000000.0, flat), axis=-1)

            def expert(muW, gW, gqa, gqb, gs, uW, uqa, uqb, us, dW, dqa, dqb, ds, w):
                xe = x + w @ muW.T
                gate = jax.nn.silu(_fused_linear(xe, gW, gqa, gqb, gs, w))
                up = _fused_linear(xe, uW, uqa, uqb, us, w)
                return _fused_linear(gate * up, dW, dqa, dqb, ds, w)
            outs = jax.vmap(expert, in_axes=(0,) * 13 + (1,))(mask_up_W, gate_W, gate_qa, gate_qb, gate_scale, up_W, up_qa, up_qb, up_scale, down_W, down_qa, down_qb, down_scale, soft)
            y = jnp.einsum('fth,tf->th', outs, scalar).reshape(b, s, h)
            sh = jax.nn.silu(hidden_states @ sh_gate_W.T) * (hidden_states @ sh_up_W.T) @ sh_down_W.T
            return y + sh
        key = jax.random.key(seed)
        ks = jax.random.split(key, 20)
        g = lambda k, shape, s=0.02: jax.random.normal(k, shape, jnp.float32) * s
        return {'hidden_states': jax.random.normal(ks[0], (B, S, H), jnp.float32), 'gate_weight': g(ks[1], (E, H)), 'inv_mapping': jnp.arange(E, dtype=jnp.int32).reshape(F, K), 'mask_up_W': g(ks[2], (F, H, K)), 'gate_W': g(ks[3], (F, I, H)), 'gate_qa': g(ks[4], (F, K, R, H)), 'gate_qb': g(ks[5], (F, K, I, R)), 'gate_scale': jnp.full((F, I), 0.1, jnp.float32), 'up_W': g(ks[6], (F, I, H)), 'up_qa': g(ks[7], (F, K, R, H)), 'up_qb': g(ks[8], (F, K, I, R)), 'up_scale': jnp.full((F, I), 0.1, jnp.float32), 'down_W': g(ks[9], (F, H, I)), 'down_qa': g(ks[10], (F, K, R, I)), 'down_qb': g(ks[11], (F, K, H, R)), 'down_scale': jnp.full((F, H), 0.1, jnp.float32), 'sh_gate_W': g(ks[12], (ISH, H)), 'sh_up_W': g(ks[13], (ISH, H)), 'sh_down_W': g(ks[14], (H, ISH))}
    _L0_ffn_in = _L0_ffn_setup()
    _d = {'L0_attn_x': _L0_attn_in['x'], 'L0_attn_W_in': _L0_attn_in['W_in'], 'L0_attn_b_in': _L0_attn_in['b_in'], 'L0_attn_W_gx': _L0_attn_in['W_gx'], 'L0_attn_b_gx': _L0_attn_in['b_gx'], 'L0_attn_W_ga': _L0_attn_in['W_ga'], 'L0_attn_b_ga': _L0_attn_in['b_ga'], 'L0_attn_a_real': _L0_attn_in['a_real'], 'L0_attn_a_imag': _L0_attn_in['a_imag'], 'L0_attn_W_out': _L0_attn_in['W_out'], 'L0_attn_b_out': _L0_attn_in['b_out'], 'L0_ffn_gate_weight': _L0_ffn_in['gate_weight'], 'L0_ffn_inv_mapping': _L0_ffn_in['inv_mapping'], 'L0_ffn_mask_up_W': _L0_ffn_in['mask_up_W'], 'L0_ffn_gate_W': _L0_ffn_in['gate_W'], 'L0_ffn_gate_qa': _L0_ffn_in['gate_qa'], 'L0_ffn_gate_qb': _L0_ffn_in['gate_qb'], 'L0_ffn_gate_scale': _L0_ffn_in['gate_scale'], 'L0_ffn_up_W': _L0_ffn_in['up_W'], 'L0_ffn_up_qa': _L0_ffn_in['up_qa'], 'L0_ffn_up_qb': _L0_ffn_in['up_qb'], 'L0_ffn_up_scale': _L0_ffn_in['up_scale'], 'L0_ffn_down_W': _L0_ffn_in['down_W'], 'L0_ffn_down_qa': _L0_ffn_in['down_qa'], 'L0_ffn_down_qb': _L0_ffn_in['down_qb'], 'L0_ffn_down_scale': _L0_ffn_in['down_scale'], 'L0_ffn_sh_gate_W': _L0_ffn_in['sh_gate_W'], 'L0_ffn_sh_up_W': _L0_ffn_in['sh_up_W'], 'L0_ffn_sh_down_W': _L0_ffn_in['sh_down_W']}
    _x0 = _d['L0_attn_x']
    _d['L0_attn_x'] = jax.random.normal(jax.random.fold_in(jax.random.key(seed), 1), (2, 2048, 256), dtype=_x0.dtype)
    del _x0
    return _d

def reference(L0_attn_x, L0_attn_W_in, L0_attn_b_in, L0_attn_W_gx, L0_attn_b_gx, L0_attn_W_ga, L0_attn_b_ga, L0_attn_a_real, L0_attn_a_imag, L0_attn_W_out, L0_attn_b_out, L0_ffn_gate_weight, L0_ffn_inv_mapping, L0_ffn_mask_up_W, L0_ffn_gate_W, L0_ffn_gate_qa, L0_ffn_gate_qb, L0_ffn_gate_scale, L0_ffn_up_W, L0_ffn_up_qa, L0_ffn_up_qb, L0_ffn_up_scale, L0_ffn_down_W, L0_ffn_down_qa, L0_ffn_down_qb, L0_ffn_down_scale, L0_ffn_sh_gate_W, L0_ffn_sh_up_W, L0_ffn_sh_down_W):

    def _L0_attn_ref(x, W_in, b_in, W_gx, b_gx, W_ga, b_ga, a_real, a_imag, W_out, b_out):
        import jax, jax.numpy as jnp
        import numpy as np
        B, T, D_IN = (8, 512, 256)
        D_HIDDEN = 256
        D_OUT = 256
        N_BLOCKS = 8
        R_MIN, R_MAX = (0.9, 0.999)
        INIT_IMAG = 0.1

        def _lecun(key, shape, fan_in):
            return (jax.random.normal(key, shape, dtype=jnp.float32) * np.sqrt(1.0 / fan_in)).astype(jnp.float32)

        def _block_diag_linear(x, W, b):
            h, i, j = W.shape
            xb = x.reshape(x.shape[0], x.shape[1], h, i)
            y = jnp.einsum('bthi,hij->bthj', xb, W) + b
            return y.reshape(y.shape[0], y.shape[1], h * j)

        def _linear_scan(a, x):

            def combine(l, r):
                al, bl = l
                ar, br = r
                return (al * ar, ar * bl + br)
            _, h = jax.lax.associative_scan(combine, (a, x), axis=1)
            return h

        def _reference_tuple_inner(x, W_in, b_in, W_gx, b_gx, W_ga, b_ga, a_real, a_imag, W_out, b_out):
            xh = x @ W_in + b_in
            gate_x = jax.nn.sigmoid(_block_diag_linear(xh, W_gx, b_gx))
            gate_a = jax.nn.sigmoid(_block_diag_linear(xh, W_ga, b_ga))
            log_a_re = -8.0 * gate_a * jax.nn.softplus(a_real)
            log_a_im = a_imag * gate_a
            a = jnp.exp(jax.lax.complex(log_a_re, log_a_im))
            a_sq = jnp.exp(jax.lax.complex(2.0 * log_a_re, 2.0 * log_a_im))
            xr, xi = jnp.split(xh, 2, axis=-1)
            xc = jax.lax.complex(xr, xi) * gate_x
            xc = jnp.sqrt(1.0 - a_sq) * xc
            h = _linear_scan(a, xc)
            h_m = jnp.concatenate([h.real, h.imag], axis=-1)
            out = h_m @ W_out + b_out
            h_last = h_m[:, -1]
            return (out, h_last)
        return _reference_tuple_inner(x, W_in, b_in, W_gx, b_gx, W_ga, b_ga, a_real, a_imag, W_out, b_out)[0]

    def _L0_ffn_ref(hidden_states, gate_weight, inv_mapping, mask_up_W, gate_W, gate_qa, gate_qb, gate_scale, up_W, up_qa, up_qb, up_scale, down_W, down_qa, down_qb, down_scale, sh_gate_W, sh_up_W, sh_down_W):
        import jax, jax.numpy as jnp
        import numpy as np
        B, S, H, I, E, F, K, R, TOPK = (1, 128, 256, 176, 64, 8, 8, 8, 6)
        ISH = 2 * I

        def _fused_linear(x, W, qa, qb, scale, w):
            out = x @ W.T
            a = jnp.einsum('th,krh->tkr', x, qa)
            b = jnp.einsum('tkr,khr->tkh', a, qb)
            mix = jnp.einsum('tkh,tk->th', b, w)
            return out + scale[None, :] * mix

        def _moe_forward(hidden_states, gate_weight, inv_mapping, mask_up_W, gate_W, gate_qa, gate_qb, gate_scale, up_W, up_qa, up_qb, up_scale, down_W, down_qa, down_qb, down_scale, sh_gate_W, sh_up_W, sh_down_W):
            b, s, h = hidden_states.shape
            x = hidden_states.reshape(-1, h)
            T = x.shape[0]
            scores = jax.nn.softmax(x @ gate_weight.T, axis=-1)
            topk_w, topk_idx = jax.lax.top_k(scores, TOPK)
            w_dense = jnp.zeros((T, E), x.dtype).at[jnp.arange(T)[:, None], topk_idx].add(topk_w)
            flat = w_dense[:, inv_mapping]
            scalar = flat.sum(-1)
            soft = jax.nn.softmax(jnp.where(flat == 0, -1000000000.0, flat), axis=-1)

            def expert(muW, gW, gqa, gqb, gs, uW, uqa, uqb, us, dW, dqa, dqb, ds, w):
                xe = x + w @ muW.T
                gate = jax.nn.silu(_fused_linear(xe, gW, gqa, gqb, gs, w))
                up = _fused_linear(xe, uW, uqa, uqb, us, w)
                return _fused_linear(gate * up, dW, dqa, dqb, ds, w)
            outs = jax.vmap(expert, in_axes=(0,) * 13 + (1,))(mask_up_W, gate_W, gate_qa, gate_qb, gate_scale, up_W, up_qa, up_qb, up_scale, down_W, down_qa, down_qb, down_scale, soft)
            y = jnp.einsum('fth,tf->th', outs, scalar).reshape(b, s, h)
            sh = jax.nn.silu(hidden_states @ sh_gate_W.T) * (hidden_states @ sh_up_W.T) @ sh_down_W.T
            return y + sh
        return _moe_forward(hidden_states, gate_weight, inv_mapping, mask_up_W, gate_W, gate_qa, gate_qb, gate_scale, up_W, up_qa, up_qb, up_scale, down_W, down_qa, down_qb, down_scale, sh_gate_W, sh_up_W, sh_down_W)
    x = L0_attn_x
    x = x + _layernorm(_L0_attn_ref(_layernorm(x, axis=-1), L0_attn_W_in, L0_attn_b_in, L0_attn_W_gx, L0_attn_b_gx, L0_attn_W_ga, L0_attn_b_ga, L0_attn_a_real, L0_attn_a_imag, L0_attn_W_out, L0_attn_b_out), axis=-1)
    x = x + _layernorm(_L0_ffn_ref(_layernorm(x, axis=-1), L0_ffn_gate_weight, L0_ffn_inv_mapping, L0_ffn_mask_up_W, L0_ffn_gate_W, L0_ffn_gate_qa, L0_ffn_gate_qb, L0_ffn_gate_scale, L0_ffn_up_W, L0_ffn_up_qa, L0_ffn_up_qb, L0_ffn_up_scale, L0_ffn_down_W, L0_ffn_down_qa, L0_ffn_down_qb, L0_ffn_down_scale, L0_ffn_sh_gate_W, L0_ffn_sh_up_W, L0_ffn_sh_down_W), axis=-1)
    return x

_drawn_inputs = setup_inputs


def setup_inputs(seed=0):
    import zlib

    import numpy as np

    out = dict(_drawn_inputs(seed))
    spreads = {'L0_attn_b_in': (0.0, 0.1),
     'L0_attn_b_out': (0.0, 0.1),
     'L0_ffn_gate_scale': (0.10000000149011612, 0.6),
     'L0_ffn_up_scale': (0.10000000149011612, 0.6),
     'L0_ffn_down_scale': (0.10000000149011612, 0.6)}
    factors = {'L0_ffn_mask_up_W': 47.249,
     'L0_ffn_gate_qa': 8.0,
     'L0_ffn_gate_qb': 8.0,
     'L0_ffn_up_qa': 23.291,
     'L0_ffn_up_qb': 22.812,
     'L0_ffn_down_qa': 21.643,
     'L0_ffn_down_qb': 21.411}
    for name, (base, spread) in spreads.items():
        noise = np.random.default_rng([zlib.crc32(name.encode()), seed]).standard_normal(out[name].shape)
        drawn = base * np.exp(spread * noise) if base else spread * noise
        out[name] = jnp.asarray(drawn.astype(out[name].dtype))
    for name, factor in factors.items():
        out[name] = (out[name] * factor).astype(out[name].dtype)
    return out
```

```python
import math
from contextlib import ExitStack

import numpy as np
import concourse.bass as bass
from concourse import mybir

F32, F32R, I32 = mybir.dt.float32, mybir.dt.float32r, mybir.dt.int32
ALU, ACT, AX = mybir.AluOpType, mybir.ActivationFunctionType, mybir.AxisListType

P = 128
B, S, H = 2, 2048, 256
KH = H // P
HALF = 256
TOK = B * HALF
NT = S // HALF
SUB = TOK // P
F, K, R, I = 8, 8, 8, 176
E = F * K
PAIRS = F // 2
IR = I - P
ISH = 2 * I
TOP = 6
WIDTH = [P, P, 2 * IR]
COL = [0, P, 2 * P]
GU = 2 * (2 * P + 2 * IR) + 2 * P
UP0 = 2 * P + 2 * IR
LR0 = 2 * UP0
CHUNK = GU // 2
QCOL = [0, 0, P]
QUP = P + 2 * IR
SW = [P, P, ISH - 2 * P]
EPS = 1e-5
ROUND1 = 1.5 * 2.0 ** 23
ROUND12 = 1.5 * 2.0 ** 11
TWO_PI = 6.2831850
TINY = 1e-30
OFF = -1e9


def build(nc, A, steps):
    ctx = ExitStack()
    with ctx:
        def sb(name, shape, dt=F32):
            return ctx.enter_context(nc.sbuf_tensor(name, shape, dt))

        def bank(name):
            return ctx.enter_context(nc.psum_tensor(name, [P, 512], F32))

        def sem(name):
            return ctx.enter_context(nc.semaphore(name))

        gu_hi, gu_lo = sb("gu_hi", [P, PAIRS, KH, GU], F32R), sb("gu_lo", [P, PAIRS, KH, GU], F32R)
        sgu_hi, sgu_lo = sb("sgu_hi", [P, KH, 2 * ISH], F32R), sb("sgu_lo", [P, KH, 2 * ISH], F32R)
        mask_w = sb("mask_w", [P, 2, GU], F32R)
        router_hi, router_lo = sb("router_hi", [P, KH * E], F32R), sb("router_lo", [P, KH * E], F32R)
        select = sb("select", [P, 3 * P + 2 * IR], F32R)
        qb = sb("qb", [P, PAIRS, 2 * QUP])
        down = sb("down", [P, PAIRS, 3, H])
        dqa = sb("dqa", [P, PAIRS, 5 * 64])
        dqb = sb("dqb", [P, PAIRS, H])
        sdown = sb("sdown", [P, 3, H])
        w_in, w_gate, w_out = sb("w_in", [P, KH, H]), sb("w_gate", [P, KH, H]), sb("w_out", [P, KH, H])
        ident, onehot = sb("ident", [P, P]), sb("onehot", [P, E])
        inv_f = sb("inv_f", [P, E])
        inv_i = sb("inv_i", [P, E], I32)
        expert_row = sb("expert_row", [P, 1])
        b_in, b_gate, a_par = sb("b_in", [P, 2]), sb("b_gate", [P, 2]), sb("a_par", [P, 2])
        half_bg, decay, turns, prep = sb("half_bg", [P, 2]), sb("decay", [P, 1]), sb("turns", [P, 1]), sb("prep", [P, 4])
        consts = sb("consts", [P, 2])
        b_out, ones_row = sb("b_out", [1, H]), sb("ones_row", [1, P])
        ones = sb("ones", [P, 1])

        x_in = sb("x_in", [P, B, 2, H])
        x1 = sb("x1", [P, B, 2, H])
        xn2 = sb("xn2", [P, B, 2, H])
        res = sb("res", [P, SUB, H])
        xn = sb("xn", [P, 2, H])
        xt = sb("xt", [P, 2, HALF])
        xh = sb("xh", [P, 2, HALF])
        tg = sb("tg", [P, HALF])
        gt = sb("gt", [P, 2, HALF])
        ph = sb("ph", [P, 2, HALF])
        sn, cs = sb("sn", [P, 2, HALF]), sb("cs", [P, 2, HALF])
        w = [sb(f"w{i}", [P, HALF]) for i in range(4)]
        rad = sb("rad", [P, HALF])
        pw = [sb(f"pw{i}", [P, HALF]) for i in range(3)]
        carry = sb("carry", [P, B, 4])
        bn1, bn2, bn3, bn4 = (sb(f"bn{i}", [P, 4, 6]) for i in range(1, 5))
        mv1, mv2, mv3, mv4 = (sb(f"mv{i}", [P, 4, 2]) for i in range(1, 5))
        powers, var_eps = sb("powers", [P, 2, 4]), sb("var_eps", [P, 4])
        rs1, rs2, rs3, rs4 = (sb(f"rs{i}", [P, 4]) for i in range(1, 5))
        nm4, spare = sb("nm4", [P, 4]), sb("spare", [P, 1])

        logit = w[0][:].rearrange("p (s e) -> p s e", e=E)
        soft, flat = w[1], w[2]
        chosen = w[3][:].rearrange("p (s e) -> p s e", e=E)
        chosen_t = xn[:, 0, :]
        rmax, rsum, rinv = sb("rmax", [P, SUB]), sb("rsum", [P, SUB]), sb("rinv", [P, SUB])
        score, left = sb("score", [P, SUB, E + 2]), sb("left", [P, SUB, E + 2])
        top8 = sb("top8", [P, SUB, 8])
        gmax, gsum, ginv, scal = (sb(n, [P, SUB * F]) for n in ("gmax", "gsum", "ginv", "scal"))
        stack_tm = sb("stack_tm", [P, SUB, PAIRS, 64], F32R)

        x2_hi, x2_lo = sb("x2_hi", [P, KH, TOK], F32R), sb("x2_lo", [P, KH, TOK], F32R)
        stack = sb("stack", [P, 2, TOK], F32R)
        tmp = [sb(f"tmp{i}", [P, TOK]) for i in range(3)]
        hid = [sb(f"hid{i}", [P, TOK]) for i in range(3)]
        lr_g, lr_u, lr_d = sb("lr_g", [P, TOK]), sb("lr_u", [P, TOK]), sb("lr_d", [P, TOK])
        wrep = [sb(f"wrep{i}", [P, TOK]) for i in range(2)]
        y_sb = wrep

        bank_a, bank_b = bank("bank_a"), bank("bank_b")
        bank_r, bank_g, bank_u, bank_d = bank("bank_r"), bank("bank_g"), bank("bank_u"), bank("bank_d")
        bank_y = [bank("bank_y0"), bank("bank_y1")]

        S_ = {}
        def named(*names):
            for n in names:
                S_[n] = sem(n)
            return [S_[n] for n in names]
        small_in, chunk_in0, chunk_in1, chunk_in2, chunk_in3, scale_in, pmask_in, wts_in = named(
            "small_in", "chunk_in0", "chunk_in1", "chunk_in2", "chunk_in3", "scale_in", "pmask_in", "wts_in")
        chunk_in = [chunk_in0, chunk_in1, chunk_in2, chunk_in3]
        chunk_hi, chunk_lo, mask_full, mask_done, scaled, prep_e, prep_l, prep_done = named(
            "chunk_hi", "chunk_lo", "mask_full", "mask_done", "scaled", "prep_e", "prep_l", "prep_done")
        x_loaded0, x_loaded1, x_used = named("x_loaded0", "x_loaded1", "x_used")
        x_loaded = [x_loaded0, x_loaded1]
        var1, rs1_ready, xn_ready, xt_full, xt_ready, xh_full, xh_ready = named(
            "var1", "rs1_ready", "xn_ready", "xt_full", "xt_ready", "xh_full", "xh_ready")
        gates_full, gates_read, ga_ready, tanh_ready, ph_ready, trig_ready = named(
            "gates_full", "gates_read", "ga_ready", "tanh_ready", "ph_ready", "trig_ready")
        pq_ready, sq_ready, norm2_ready, norm_ready, mp_ready, sr_ready, fac_ready = named(
            "pq_ready", "sq_ready", "norm2_ready", "norm_ready", "mp_ready", "sr_ready", "fac_ready")
        mr_ready, mi_ready, bi_ready, g_ready, hr_ready, hi_ready, out_full, out_read = named(
            "mr_ready", "mi_ready", "bi_ready", "g_ready", "hr_ready", "hi_ready", "out_full", "out_read")
        var2, rs2_ready, var3, rs3_ready, xn2_ready = named("var2", "rs2_ready", "var3", "rs3_ready", "xn2_ready")
        x2t_full, x2h_ready, x2l_ready, rt_full, rt_read, exp_ready, chosen_ready, ct_full, ct_ready = named(
            "x2t_full", "x2h_ready", "x2l_ready", "rt_full", "rt_read", "exp_ready", "chosen_ready", "ct_full",
            "ct_ready")
        flat_full, flat_read, shifted, soft_exp, stm_ready, st_full, st_copied = named(
            "flat_full", "flat_read", "shifted", "soft_exp", "stm_ready", "st_full", "st_copied")
        gate_full, up_full, silu_done, hid_done, srep_full, srep_taken, wrep_full, wrep_taken = named(
            "gate_full", "up_full", "silu_done", "hid_done", "srep_full", "srep_taken", "wrep_full", "wrep_taken")
        mask_added, lrg_full, lru_full, lrd_full, lrg_done, lru_done, lrd_done, sdown_used, pair_done = named(
            "mask_added", "lrg_full", "lru_full", "lrd_full", "lrg_done", "lru_done", "lrd_done", "sdown_used", "pair_done")
        y_copied, yt_full, var4, rs4_ready, yt_read, final_ready, res_copied, stored = named(
            "y_copied", "yt_full", "var4", "rs4_ready", "yt_read", "final_ready", "res_copied", "stored")
        dve_step, act_step, pool_step = named("dve_step", "act_step", "pool_step")

        block = ctx.enter_context(nc.Block())

        def wait(eng, s, value):
            if not (isinstance(value, int) and value <= 0):
                eng.wait_ge(s, value)

        class Steps:
            def __init__(self, eng, s, name):
                self.eng, self.sem, self.name, self.base, self.k = eng, s, name, 0, 0
                self.seen = {}

            def link(self, ins):
                self.k += 1
                ins.then_inc(self.sem, 1)
                self.eng.wait_ge(self.sem, self.base + self.k)

            def start(self, part, i=None):
                n0, n1 = steps.get((self.name, "prologue"), 0), steps.get((self.name, "turn"), 0)
                self.base = {"prologue": 0, "turn": None if i is None else n0 + (i - 1) * n1,
                             "epilogue": n0 + (NT - 1) * n1}[part]
                self.k, self.part = 0, part

            def end(self):
                self.seen[(self.name, self.part)] = self.k
                found[(self.name, self.part)] = self.k

        found = {}

        xv = A["x"].rearrange("b (t s p) d -> b t p s d", p=P, s=2)
        ov = A["out"].rearrange("b (t s p) d -> b t p s d", p=P, s=2)

        chunks = []
        for p in range(PAIRS):
            for c in range(2):
                for k in range(KH):
                    chunks.append((A["w_gu"][:, p, k, c * CHUNK:(c + 1) * CHUNK], gu_hi[:, p, k, c * CHUNK:(c + 1) * CHUNK],
                                   gu_lo[:, p, k, c * CHUNK:(c + 1) * CHUNK], CHUNK))
        for k in range(KH):
            for c in range(2):
                chunks.append((A["w_sgu"][:, k, c * ISH:(c + 1) * ISH], sgu_hi[:, k, c * ISH:(c + 1) * ISH],
                               sgu_lo[:, k, c * ISH:(c + 1) * ISH], ISH))
        chunks.append((A["w_router"], router_hi[:, :], router_lo[:, :], KH * E))
        NCH = len(chunks)
        raw = [tmp[0], tmp[1], tmp[2], hid[0]]
        NRAW = len(raw)
        mask_tmp, pattern = hid[1], res[:, :, :].rearrange("p s d -> p (s d)")

        @block.sync
        def _(sp):
            for b in range(B):
                sp.dma_start(x_in[:, b], xv[b, 0]).then_inc(x_loaded[b], 16)
            for dst, src in ((ident, "ident"), (w_in, "w_in"), (w_gate, "w_gate"), (w_out, "w_out"), (b_in, "b_in"),
                             (b_gate, "b_gate"), (a_par, "a_par"), (b_out, "b_out"), (inv_i, "inv"),
                             (expert_row, "expert_row"), (hid[2], "mask_up")):
                d = dst[:, :] if len(dst.shape) == 2 else dst[:, :, :]
                sp.dma_start(d, A[src]).then_inc(small_in, 16)
            sp.dma_start(lr_g[:, 0:3 * P + 2 * IR], A["select"]).then_inc(small_in, 16)
            sp.dma_start(pattern[:, 0:GU], A["pattern"]).then_inc(pmask_in, 16)
            for n, (src, _, _, cols) in enumerate(chunks):
                if n >= NRAW:
                    sp.wait_ge(chunk_lo, n - NRAW + 1)
                    if n - NRAW < 4 * PAIRS:
                        sp.wait_ge(mask_full, (n - NRAW) // 2 + 1)
                sp.dma_start(raw[n % NRAW][:, 0:cols], src).then_inc(chunk_in[n % NRAW], 16)

            def load(T):
                for b in range(B):
                    sp.wait_ge(x_used, 2 * T - 1 + b)
                    sp.dma_start(x_in[:, b], xv[b, T]).then_inc(x_loaded[b], 16)

            def store(t):
                sp.wait_ge(final_ready, t + 1)
                for b in range(B):
                    sp.dma_start(ov[b, t], res[:, 2 * b:2 * b + 2, :]).then_inc(stored, 16)

            load(1)
            store(0)
            with sp.Fori(2, NT) as T:
                load(T)
                store(T - 1)
            store(NT - 1)
            sp.wait_ge(stored, 32 * NT)

        @block.tensor
        def _(pe):
            def mm(out, lhs, rhs, start, stop):
                return nc.tensor.matmul(out, lhs, rhs, start=start, stop=stop, skip_group_check=True)

            def split3(out, hi, lo, rhs_hi, rhs_lo, start, stop=False):
                mm(out, hi, rhs_hi, start, False)
                mm(out, hi, rhs_lo, False, False)
                return mm(out, lo, rhs_hi, False, stop)

            def turn(out, src, rows=P):
                return nc.tensor.transpose(out, src, ident[0:rows, 0:rows])

            def t1(T, b):
                n = 2 * T + b
                wait(pe, xn_ready, n + 1)
                if b == 0:
                    wait(pe, st_copied, 2 * T)
                else:
                    wait(pe, out_read, n)
                for k in range(KH):
                    for s in range(2):
                        last = turn(bank_a[:, k * HALF + s * P:k * HALF + (s + 1) * P], xn[:, s, k * P:(k + 1) * P])
                last.then_inc(xt_full, 1)

            def xh_mm(T, b):
                n = 2 * T + b
                wait(pe, xt_ready, n + 1)
                if b:
                    wait(pe, xh_ready, 2 * n)
                for m in range(2):
                    for k in range(KH):
                        last = mm(bank_b[:, m * HALF:(m + 1) * HALF], w_in[:, k, m * P:(m + 1) * P], xt[:, k, :],
                                  k == 0, k == KH - 1)
                last.then_inc(xh_full, 1)

            def gates_mm(T, b):
                n = 2 * T + b
                wait(pe, xh_ready, 2 * (n + 1))
                for m in range(2):
                    for k in range(KH):
                        last = mm(bank_a[:, m * HALF:(m + 1) * HALF], w_gate[:, k, m * P:(m + 1) * P], xh[:, k, :],
                                  k == 0, k == KH - 1)
                last.then_inc(gates_full, 1)

            def out_mm(T, b):
                n = 2 * T + b
                wait(pe, gates_read, 2 * (n + 1))
                wait(pe, hr_ready, n + 1)
                wait(pe, hi_ready, n + 1)
                for s in range(2):
                    o = bank_a[:, s * H:(s + 1) * H]
                    mm(o, ones_row[:, :], b_out[:, :], True, False)
                    for k in range(KH):
                        last = mm(o, xt[:, k, s * P:(s + 1) * P], w_out[:, k, :], False, k == KH - 1)
                last.then_inc(out_full, 1)

            def pe_hook(q, part, T):
                p, j = divmod(q, 3)
                b = p // 2
                if (p % 2, j, part) == (0, 0, 0):
                    t1(T, b)
                if (p % 2, j, part) == (0, 0, 1):
                    xh_mm(T, b)
                if (p % 2, j, part) == (0, 1, 0):
                    gates_mm(T, b)
                if (p % 2, j, part) == (1, 2, 0):
                    out_mm(T, b)

            def x2_turn(T):
                wait(pe, xn2_ready, 2 * T + 2)
                wait(pe, out_read, 2 * T + 2)
                for k, o in enumerate((bank_a, bank_b)):
                    for b in range(B):
                        for s in range(2):
                            last = turn(o[:, (2 * b + s) * P:(2 * b + s + 1) * P], xn2[:, b, s, k * P:(k + 1) * P])
                    last.then_inc(x2t_full, 1)

            def router_mm(T):
                wait(pe, x2h_ready, 2 * T + 2)
                wait(pe, x2l_ready, 2 * T + 2)
                for s in range(SUB):
                    o = bank_a[:, s * E:(s + 1) * E]
                    for k in range(KH):
                        hi, lo = x2_hi[:, k, s * P:(s + 1) * P], x2_lo[:, k, s * P:(s + 1) * P]
                        wh, wl = router_hi[:, k * E:(k + 1) * E], router_lo[:, k * E:(k + 1) * E]
                        mm(o, hi, wh, k == 0, False)
                        mm(o, lo, wh, False, False)
                        last = mm(o, hi, wl, False, k == KH - 1)
                last.then_inc(rt_full, 1)

            def chosen_turn(T):
                wait(pe, chosen_ready, T + 1)
                for g in range(SUB // 2):
                    last = turn(bank_b[:, g * P:(g + 1) * P], w[3][:, g * P:(g + 1) * P])
                last.then_inc(ct_full, 1)

            def flat_mm(T):
                wait(pe, ct_ready, T + 1)
                wait(pe, rt_read, T + 1)
                for s in range(SUB):
                    last = mm((bank_a, bank_b)[s % 2][:, (s // 2) * E:(s // 2 + 1) * E],
                              chosen_t[E * (s % 2):E * (s % 2 + 1), (s // 2) * P:(s // 2 + 1) * P],
                              onehot[E * (s % 2):E * (s % 2 + 1), :], True, True)
                last.then_inc(flat_full, 1)

            def y_turn(t, T):
                wait(pe, y_copied, 2 * t + 2)
                wait(pe, flat_read, 2 * T)
                for g, o in enumerate((bank_a, bank_b)):
                    for s in range(2):
                        for k in range(KH):
                            last = turn(o[:, s * H + k * P:s * H + (k + 1) * P],
                                        y_sb[k][:, (2 * g + s) * P:(2 * g + s + 1) * P])
                    last.then_inc(yt_full, 1)

            def stack_turn(T):
                wait(pe, stm_ready, T + 1)
                wait(pe, yt_read, T)
                for c, o in enumerate((bank_a, bank_b)):
                    for s in range(SUB):
                        last = turn(o[:, s * P:(s + 1) * P],
                                    stack_tm[:, s, 2 * c:2 * c + 2, :].rearrange("p a c -> p (a c)").bitcast(F32))
                    last.then_inc(st_full, 1)

            def shared_in(t, s):
                N = 15 * t + s
                m = SW[s]
                for up, (o, full) in enumerate(((bank_g, gate_full), (bank_u, up_full))):
                    wait(pe, hid_done if up else silu_done, N)
                    for k in range(KH):
                        c = up * ISH + s * P
                        last = split3(o[0:m, :], sgu_hi[:, k, c:c + m], sgu_lo[:, k, c:c + m], x2_hi[:, k, :],
                                      x2_lo[:, k, :], k == 0, k == KH - 1)
                    last.then_inc(full, 1)

            def shared_down(t):
                wait(pe, hid_done, 15 * t + 3)
                wait(pe, y_copied, 2 * t)
                for m in range(KH):
                    for j in range(3):
                        last = mm(bank_y[m][:, :], sdown[0:SW[j], j, m * P:(m + 1) * P], hid[j][0:SW[j], :], j == 0, False)
                last.then_inc(sdown_used, 1)

            def base(p):
                return 64 * (p % 2), p // 2

            def srep(t, q):
                p, j = divmod(q, 3)
                o, c = base(p)
                if j == 0:
                    wait(pe, wrep_taken, 4 * t + p + 1)
                else:
                    wait(pe, srep_taken, 12 * t + q)
                mm(bank_r[0:WIDTH[j], :], select[o:o + 64, P + COL[j]:P + COL[j] + WIDTH[j]], stack[o:o + 64, c, :],
                   True, True).then_inc(srep_full, 1)

            def in_mm(t, q, up):
                p, j = divmod(q, 3)
                o, c = base(p)
                N = 15 * t + 3 + q
                m = WIDTH[j]
                cols = slice(up * UP0 + COL[j], up * UP0 + COL[j] + m)
                out = (bank_u if up else bank_g)[0:m, :]
                if up:
                    wait(pe, hid_done, N)
                elif j == 0:
                    wait(pe, lru_done, 4 * t + p + 1)
                else:
                    wait(pe, silu_done, N)
                mm(out, mask_w[o:o + 64, c, cols], stack[o:o + 64, c, :], True, False).then_inc(mask_added, 1)
                for k in range(KH):
                    split3(out, gu_hi[:, p, k, cols], gu_lo[:, p, k, cols], x2_hi[:, k, :], x2_lo[:, k, :], False)
                wait(pe, lru_done if up else lrg_done, 4 * t + p + 1)
                wait(pe, mask_added, 24 * t + 2 * q + up + 1)
                rows = (slice(0, 64), slice(64, P), slice(0, P))[j]
                q0 = up * QUP + QCOL[j]
                mm(out, qb[rows, p, q0:q0 + m], (lr_u if up else lr_g)[rows, :], False, True)\
                    .then_inc(up_full if up else gate_full, 1)

            def low_rank_in(t, p):
                o, c = base(p)
                for up, (out, full) in enumerate(((bank_d, lrg_full), (bank_g, lru_full))):
                    if up:
                        wait(pe, silu_done, 15 * t + 3 + 3 * p)
                    elif p == 1:
                        wait(pe, lrg_done, 4 * t + 1)
                    else:
                        wait(pe, lrd_done, 4 * t + max(p - 1, 0))
                    cols = slice(LR0 + up * P, LR0 + (up + 1) * P)
                    for k in range(KH):
                        split3(out[:, :], gu_hi[:, p, k, cols], gu_lo[:, p, k, cols], x2_hi[:, k, :], x2_lo[:, k, :], k == 0)
                    if p == 0 and not up:
                        wait(pe, st_copied, 2 * t + 2)
                    mm(out[:, :], mask_w[o:o + 64, c, cols], stack[o:o + 64, c, :], False, True).then_inc(full, 1)
                    if not up:
                        wait(pe, srep_taken, 12 * t + 3 * p)
                        mm(bank_r[:, :], select[o:o + 64, 0:P], stack[o:o + 64, c, :], True, True)\
                            .then_inc(wrep_full, 1)

            def pair_down(t, p):
                for j in range(3):
                    wait(pe, hid_done, 15 * t + 3 + 3 * p + j + 1)
                    for m in range(KH):
                        mm(bank_y[m][:, :], down[0:WIDTH[j], p, j, m * P:(m + 1) * P], hid[j][0:WIDTH[j], :], False, False)
                if p < PAIRS - 1:
                    wait(pe, lrg_done, 4 * t + p + 2)
                else:
                    wait(pe, lrd_done, 4 * t + p)
                for j, c in enumerate((0, 64, 192)):
                    last = mm(bank_d[:, :], dqa[0:WIDTH[j], p, c:c + P], hid[j][0:WIDTH[j], :], j == 0, j == 2)
                last.then_inc(lrd_full, 1)

            def low_rank_out(t, p):
                wait(pe, lrd_done, 4 * t + p + 1)
                for m in range(KH):
                    last = mm(bank_y[m][:, :], dqb[:, p, m * P:(m + 1) * P], lr_d[:, :], False, p == PAIRS - 1)
                last.then_inc(pair_done, 1)

            def experts(t, T):
                low_rank_in(t, 0)
                shared_down(t)
                for q in range(12):
                    p, j = divmod(q, 3)
                    if T is not None:
                        pe_hook(q, 0, T)
                    srep(t, q)
                    in_mm(t, q, 0)
                    if T is not None:
                        pe_hook(q, 1, T)
                    in_mm(t, q, 1)
                    if j == 0 and p:
                        low_rank_out(t, p - 1)
                    if j == 2:
                        if p < PAIRS - 1:
                            low_rank_in(t, p + 1)
                        pair_down(t, p)
                if T is not None:
                    x2_turn(T)
                low_rank_out(t, PAIRS - 1)
                if T is not None:
                    router_mm(T)
                    shared_in(T, 0)
                    chosen_turn(T)
                    shared_in(T, 1)
                    flat_mm(T)
                    y_turn(t, T + 1)
                    shared_in(T, 2)
                    stack_turn(T)
                else:
                    y_turn(t, NT)

            pe.wait_ge(small_in, 16 * 12)
            pe.wait_ge(prep_done, 1)
            mask_l = hid[2][:, :].rearrange("p (k c m) -> p k c m", k=KH, c=2)

            def mask_mm(g):
                if g:
                    pe.wait_ge(mask_done, g)
                for k in range(KH):
                    n = 2 * g + k
                    pe.wait_ge(chunk_in[n % NRAW], 16 * (n // NRAW + 1))
                    last = mm(bank_y[0][:, 0:CHUNK], mask_l[:, k, g // 4, :], raw[n % NRAW][:, 0:CHUNK], k == 0, k == 1)
                last.then_inc(mask_full, 1)

            for q in range(12):
                if q < 2 * PAIRS:
                    mask_mm(q)
                for part in range(2):
                    pe_hook(q, part, 0)
            x2_turn(0)
            router_mm(0)
            chosen_turn(0)
            flat_mm(0)
            pe.wait_ge(chunk_hi, NCH)
            pe.wait_ge(chunk_lo, NCH)
            shared_in(0, 0)
            shared_in(0, 1)
            shared_in(0, 2)
            stack_turn(0)
            pe.wait_ge(mask_done, 2 * PAIRS)
            pe.wait_ge(wts_in, 16 * 5)
            pe.wait_ge(scaled, 3)
            experts(0, 1)
            with pe.Fori(2, NT) as T:
                experts(T - 1, T)
            experts(NT - 1, None)

        @block.vector
        def _(dve):
            st = Steps(dve, dve_step, "dve")
            link = st.link

            def settle():
                dve.memset(spare[:], 0.0)

            def norm_stats(bn, mv, srcs, signal):
                for i, src in enumerate(srcs):
                    last = dve.bn_stats(bn[:, i, :], src)
                link(last)
                settle()
                for i in range(len(srcs)):
                    last = dve.bn_aggr(mv[:, i, :], bn[:, i, :])
                last.then_inc(signal, 1)


            def ln1(T, b):
                n = 2 * T + b
                wait(dve, x_loaded[b], 16 * (T + 1))
                norm_stats(bn1, mv1, [x_in[:, b, s, :] for s in range(2)], var1)
                wait(dve, rs1_ready, n + 1)
                wait(dve, xt_full, n)
                for s in range(2):
                    last = dve.tensor_scalar(xn[:, s, :], x_in[:, b, s, :], mv1[:, s, 0:1], rs1[:, s:s + 1],
                                             ALU.subtract, ALU.mult)
                last.then_inc(xn_ready, 1)

            def e1a(T, b):
                n = 2 * T + b
                wait(dve, gates_read, 2 * (n + 1))
                ga = gt[:, 0, :]
                dve.tensor_scalar(ga, ga, 0.5, 0.5, ALU.mult, ALU.add).then_inc(ga_ready, 1)
                wait(dve, ga_ready, n + 1)
                link(dve.tensor_scalar(w[0][:], ga, turns[:, 0:1], None, ALU.mult))
                link(dve.tensor_scalar(w[1][:], w[0][:], ROUND1, ROUND1, ALU.add, ALU.subtract))
                link(dve.tensor_tensor(ph[:, 1, :], w[0][:], w[1][:], ALU.subtract))
                link(dve.tensor_scalar(w[0][:], ph[:, 1, :], ROUND12, ROUND12, ALU.add, ALU.subtract))
                link(dve.tensor_tensor(w[1][:], ph[:, 1, :], w[0][:], ALU.subtract))

            def e1b(T, b):
                dve.tensor_tensor_scan(w[2][:], ones[:].to_broadcast([P, HALF]), w[0][:], carry[:, b, 0:1], ALU.mult, ALU.add)
                link(dve.tensor_tensor_scan(w[3][:], ones[:].to_broadcast([P, HALF]), w[1][:], carry[:, b, 1:2], ALU.mult, ALU.add))
                link(dve.tensor_tensor(w[0][:], w[2][:], w[3][:], ALU.add))
                link(dve.tensor_scalar(w[1][:], w[0][:], ROUND1, ROUND1, ALU.add, ALU.subtract))
                link(dve.tensor_tensor(w[2][:], w[2][:], w[1][:], ALU.subtract))
                dve.tensor_copy(carry[:, b, 0:1], w[2][:, HALF - 1:HALF])
                dve.tensor_copy(carry[:, b, 1:2], w[3][:, HALF - 1:HALF])
                link(dve.tensor_tensor(ph[:, 0, :], w[2][:], w[3][:], ALU.add))
                dve.tensor_scalar(ph[:, 0, :], ph[:, 0, :], -0.5, 0.5, ALU.max, ALU.min).then_inc(ph_ready, 1)

            def e2a(T, b):
                n = 2 * T + b
                th = gt[:, 1, :]
                wait(dve, tanh_ready, n + 1)
                link(dve.tensor_scalar(w[0][:], th, 1.0, None, ALU.add))
                link(dve.reciprocal(w[1][:], w[0][:]))
                dve.tensor_scalar(rad[:], w[1][:], 2.0, -1.0, ALU.mult, ALU.add)
                link(dve.scalar_tensor_tensor(out=w[0][:], in0=th, scalar=4.0, in1=w[1][:], op0=ALU.mult, op1=ALU.mult))
                link(dve.tensor_tensor(w[2][:], w[0][:], w[1][:], ALU.mult))

            def e2b(T, b):
                n = 2 * T + b
                wait(dve, trig_ready, n + 1)
                dve.tensor_tensor(w[0][:], rad[:], sn[:, 1, :], ALU.mult)
                link(dve.tensor_tensor(w[1][:], rad[:], cs[:, 1, :], ALU.mult))
                link(dve.scalar_tensor_tensor(out=w[3][:], in0=w[0][:], scalar=2.0, in1=w[0][:], op0=ALU.mult, op1=ALU.mult))
                dve.scalar_tensor_tensor(out=gt[:, 1, :], in0=w[0][:], scalar=2.0, in1=w[1][:], op0=ALU.mult, op1=ALU.mult)
                dve.tensor_tensor(gt[:, 0, :], w[3][:], w[2][:], ALU.add).then_inc(pq_ready, 1)
                dve.tensor_scalar(tg[:], tg[:], 0.5, 0.5, ALU.mult, ALU.add)
                wait(dve, sq_ready, n + 1)
                dve.tensor_tensor(w[0][:], ph[:, 0, :], ph[:, 1, :], ALU.add).then_inc(norm2_ready, 1)
                wait(dve, norm_ready, n + 1)
                dve.tensor_tensor(w[2][:], w[1][:], gt[:, 0, :], ALU.add).then_inc(mp_ready, 1)

            def e3(T, b):
                n = 2 * T + b
                wait(dve, sr_ready, n + 1)
                link(dve.tensor_scalar(w[0][:], w[3][:], 2.0, TINY, ALU.mult, ALU.max))
                link(dve.reciprocal(w[1][:], w[0][:]))
                link(dve.tensor_tensor(w[2][:], gt[:, 1, :], w[1][:], ALU.mult))
                dve.tensor_tensor(gt[:, 0, :], w[3][:], tg[:], ALU.mult)
                dve.tensor_tensor(gt[:, 1, :], w[2][:], tg[:], ALU.mult).then_inc(fac_ready, 1)

            def e4a(T, b):
                n = 2 * T + b
                wait(dve, fac_ready, n + 1)
                s, c = sn[:, 0, :], cs[:, 0, :]
                dve.tensor_tensor(w[0][:], gt[:, 0, :], c, ALU.mult)
                link(dve.tensor_tensor(w[1][:], gt[:, 1, :], s, ALU.mult))
                dve.tensor_tensor(w[2][:], w[0][:], w[1][:], ALU.subtract).then_inc(mr_ready, 1)

            def e4b(T, b):
                n = 2 * T + b
                wait(dve, mr_ready, n + 1)
                dve.tensor_tensor(w[0][:], xh[:, 0, :], w[2][:], ALU.mult)
                wait(dve, mi_ready, n + 1)
                link(dve.tensor_tensor(w[1][:], xh[:, 1, :], pw[2][:], ALU.mult))
                link(dve.tensor_tensor(w[3][:], w[0][:], w[1][:], ALU.add))
                link(dve.tensor_tensor_scan(w[0][:], rad[:], w[3][:], carry[:, b, 2:3], ALU.mult, ALU.add))

            def e4c(T, b):
                n = 2 * T + b
                s, c = sn[:, 0, :], cs[:, 0, :]
                wait(dve, bi_ready, n + 1)
                dve.tensor_tensor_scan(w[1][:], rad[:], pw[0][:], carry[:, b, 3:4], ALU.mult, ALU.add)\
                   .then_inc(g_ready, 1)
                wait(dve, g_ready, n + 1)
                dve.tensor_copy(carry[:, b, 2:3], w[0][:, HALF - 1:HALF])
                dve.tensor_copy(carry[:, b, 3:4], w[1][:, HALF - 1:HALF])
                dve.tensor_tensor(w[2][:], w[0][:], c, ALU.mult)
                link(dve.tensor_tensor(w[3][:], w[1][:], s, ALU.mult))
                dve.tensor_tensor(xt[:, 0, :], w[2][:], w[3][:], ALU.subtract).then_inc(hr_ready, 1)

            def e6a(T, b):
                n = 2 * T + b
                wait(dve, out_full, n + 1)
                norm_stats(bn2, mv2, [bank_a[:, s * H:(s + 1) * H] for s in range(2)], var2)

            def e6b(T, b):
                n = 2 * T + b
                wait(dve, rs2_ready, n + 1)
                wait(dve, res_copied, T)
                for s in range(2):
                    last = dve.tensor_scalar(x1[:, b, s, :], bank_a[:, s * H:(s + 1) * H], mv2[:, s, 0:1],
                                             rs2[:, s:s + 1], ALU.subtract, ALU.mult)
                last.then_inc(out_read, 1)
                wait(dve, out_read, n + 1)
                dve.tensor_tensor(x1[:, b], x1[:, b], x_in[:, b], ALU.add).then_inc(x_used, 1)
                wait(dve, x_used, n + 1)
                norm_stats(bn3, mv3, [x1[:, b, s, :] for s in range(2)], var3)

            def e6c(T, b):
                n = 2 * T + b
                wait(dve, rs3_ready, n + 1)
                wait(dve, x2t_full, 2 * T)
                for s in range(2):
                    last = dve.tensor_scalar(xn2[:, b, s, :], x1[:, b, s, :], mv3[:, s, 0:1], rs3[:, s:s + 1],
                                             ALU.subtract, ALU.mult)
                last.then_inc(xn2_ready, 1)

            def dve_hook(slot, T):
                b, k = divmod(slot, 16)
                if slot == 11:
                    ln1(T, 1)
                for at, stage in ((2, e1a), (3, e1b), (5, e2a), (6, e2b), (7, e3), (8, e4a), (9, e4b), (10, e4c),
                                  (12, e6a), (13, e6b), (14, e6c)):
                    if k == at:
                        stage(T, b)

            def x2_low(T):
                wait(dve, up_full, 15 * T)
                for k, o in enumerate((bank_a, bank_b)):
                    wait(dve, x2h_ready, 2 * T + k + 1)
                    dve.tensor_tensor(x2_lo[:, k, :], o[:, :], x2_hi[:, k, :].bitcast(F32), ALU.subtract)\
                       .then_inc(x2l_ready, 1)

            def top_k(T):
                wait(dve, rt_full, T + 1)
                lg = bank_a[:, 0:SUB * E].rearrange("p (s e) -> p s e", e=E)
                link(dve.tensor_reduce(rmax[:], lg, AX.X, ALU.max))
                dve.tensor_tensor(logit, lg, rmax[:].unsqueeze(2).to_broadcast([P, SUB, E]), ALU.subtract)\
                   .then_inc(rt_read, 1)
                wait(dve, exp_ready, T + 1)
                link(dve.tensor_reduce(rsum[:], logit, AX.X, ALU.add))
                link(dve.reciprocal(rinv[:], rsum[:]))
                link(dve.tensor_tensor(score[:, :, 0:E], logit, rinv[:].unsqueeze(2).to_broadcast([P, SUB, E]), ALU.mult))
                settle()
                for s in range(SUB):
                    last = dve.max(top8[:, s, :], score[:, s, :])
                link(last)
                settle()
                for s in range(SUB):
                    last = dve.match_replace(left[:, s, :], top8[:, s, :], score[:, s, :], 0.0)
                link(last)
                wait(dve, ct_full, T)
                dve.tensor_tensor(chosen, score[:, :, 0:E], left[:, :, 0:E], ALU.subtract).then_inc(chosen_ready, 1)

            def soft_start(T):
                wait(dve, flat_full, T + 1)
                for h, o in enumerate((bank_a, bank_b)):
                    dve.tensor_copy(flat[:].rearrange("p (g h e) -> p g h e", h=2, e=E)[:, :, h, :],
                                    o[:, 0:2 * E].rearrange("p (g e) -> p g e", e=E)).then_inc(flat_read, 1)
                wait(dve, flat_read, 2 * T + 2)
                fg = flat[:].rearrange("p (g k) -> p g k", k=K)
                sg = soft[:].rearrange("p (g k) -> p g k", k=K)
                dve.tensor_reduce(scal[:], fg, AX.X, ALU.add)
                link(dve.tensor_scalar(soft[:], flat[:], 0.0, OFF, ALU.is_equal, ALU.mult))
                link(dve.tensor_tensor(soft[:], soft[:], flat[:], ALU.add))
                link(dve.tensor_reduce(gmax[:], sg, AX.X, ALU.max))
                dve.tensor_tensor(sg, sg, gmax[:].unsqueeze(2).to_broadcast([P, SUB * F, K]), ALU.subtract)\
                   .then_inc(shifted, 1)

            def soft_end(T):
                sg = soft[:].rearrange("p (g k) -> p g k", k=K)
                wait(dve, soft_exp, T + 1)
                link(dve.tensor_reduce(gsum[:], sg, AX.X, ALU.add))
                link(dve.reciprocal(ginv[:], gsum[:]))
                link(dve.tensor_tensor(sg, sg, ginv[:].unsqueeze(2).to_broadcast([P, SUB * F, K]), ALU.mult))
                wait(dve, st_full, 2 * T)
                st_v = stack_tm[:].rearrange("p s a c -> p (s a) c")
                sv = soft[:].rearrange("p (g k) -> p g k", k=2 * K)
                cv = scal[:].rearrange("p (g k) -> p g k", k=2)
                dve.tensor_copy(st_v[:, :, 48:50], cv)
                dve.tensor_copy(st_v[:, :, 32:48], sv)
                link(dve.tensor_copy(st_v[:, :, 0:16], sv))
                dve.tensor_tensor(st_v[:, :, 50:52], cv, st_v[:, :, 48:50].bitcast(F32), ALU.subtract)
                dve.tensor_tensor(st_v[:, :, 16:32], sv, st_v[:, :, 0:16].bitcast(F32), ALU.subtract)\
                   .then_inc(stm_ready, 1)

            def final(t):
                wait(dve, yt_full, 2 * t + 2)
                srcs = [(bank_a, bank_b)[s // 2][:, (s % 2) * H:(s % 2 + 1) * H] for s in range(SUB)]
                norm_stats(bn4, mv4, srcs, var4)
                wait(dve, rs4_ready, t + 1)
                wait(dve, res_copied, t + 1)
                link(dve.scalar_tensor_tensor(out=nm4[:], in0=mv4[:, :, 0], scalar=-1.0, in1=rs4[:], op0=ALU.mult, op1=ALU.mult))
                for s in range(SUB):
                    last = dve.scalar_tensor_tensor(out=res[:, s, :], in0=srcs[s], scalar=rs4[:, s:s + 1],
                                                    in1=res[:, s, :], op0=ALU.mult, op1=ALU.add)
                last.then_inc(yt_read, 1)
                wait(dve, yt_read, t + 1)
                for s in range(SUB):
                    last = dve.tensor_scalar(res[:, s, :], res[:, s, :], nm4[:, s:s + 1], None, ALU.add)
                last.then_inc(final_ready, 1)

            def hidden(t, N, m, j, scaled_by, between=None):
                wait(dve, silu_done, N + 1)
                if scaled_by is not None:
                    wait(dve, srep_full, scaled_by + 1)
                    dve.tensor_tensor(tmp[j][0:m, :], tmp[j][0:m, :], bank_r[0:m, :], ALU.mult).then_inc(srep_taken, 1)
                    if between:
                        between()
                    wait(dve, srep_taken, scaled_by + 1)
                wait(dve, up_full, N + 1)
                dve.tensor_tensor(hid[j][0:m, :], tmp[j][0:m, :], bank_u[0:m, :], ALU.mult).then_inc(hid_done, 1)

            def shared(t, s):
                hidden(t, 15 * t + s, SW[s], s, None)

            def low_rank(t, p):
                wait(dve, wrep_taken, 4 * t + p + 1)
                wait(dve, lrg_full, 4 * t + p + 1)
                dve.tensor_tensor(lr_g[:], bank_d[:, :], wrep[p % 2][:], ALU.mult).then_inc(lrg_done, 1)
                wait(dve, lru_full, 4 * t + p + 1)
                dve.tensor_tensor(lr_u[:], bank_g[:, :], wrep[p % 2][:], ALU.mult).then_inc(lru_done, 1)

            def low_rank_down(t, p):
                wait(dve, lrd_full, 4 * t + p + 1)
                wait(dve, pair_done, 4 * t + p)
                dve.tensor_tensor(lr_d[:], bank_d[:, :], wrep[p % 2][:], ALU.mult).then_inc(lrd_done, 1)

            def experts(t, T):
                if T is not None:
                    ln1(T, 0)
                low_rank(t, 0)
                for q in range(12):
                    p, j = divmod(q, 3)
                    if q == 0:
                        wait(dve, sdown_used, t + 1)
                    hook = (lambda k: dve_hook(8 * p + k, T)) if T is not None else (lambda k: None)
                    hidden(t, 15 * t + 3 + q, WIDTH[j], j, 12 * t + q, lambda: hook(2 * j))
                    hook(2 * j + 1)
                    if j == 2:
                        if p < PAIRS - 1:
                            low_rank(t, p + 1)
                        hook(6)
                        low_rank_down(t, p)
                        hook(7)
                if T is not None:
                    x2_low(T)
                    top_k(T)
                    shared(T, 0)
                    shared(T, 1)
                    soft_start(T)
                    final(t)
                    shared(T, 2)
                    soft_end(T)
                else:
                    final(t)

            st.start("prologue")
            dve.memset(carry[:], 0.0)
            dve.memset(ones[:], 1.0)
            dve.memset(ones_row[:], 1.0)
            dve.memset(score[:, :, E:E + 2], 2.0)
            dve.memset(stack_tm[:].bitcast(F32), 0.0)
            dve.memset(mask_w[:].bitcast(F32), 0.0)
            link(dve.memset(consts[:, 1:2], math.pi / 2))
            dve.wait_ge(small_in, 16 * 12)
            link(dve.tensor_scalar(prep[:, 0:1], a_par[:, 0:1], -1.0, None, ALU.mult))
            dve.tensor_tensor(prep[:, 1:2], prep[:, 0:1], a_par[:, 0:1], ALU.min).then_inc(prep_e, 1)
            dve.tensor_scalar(prep[:, 2:3], a_par[:, 0:1], 0.0, None, ALU.max)
            dve.tensor_scalar(turns[:], a_par[:, 1:2], 1.0 / (2 * math.pi), None, ALU.mult)
            dve.tensor_scalar(half_bg[:], b_gate[:], 0.5, None, ALU.mult)
            link(dve.tensor_copy(inv_f[:], inv_i[:]))
            dve.wait_ge(prep_l, 1)
            link(dve.tensor_tensor(prep[:, 2:3], prep[:, 2:3], prep[:, 3:4], ALU.add))
            dve.tensor_scalar(decay[:], prep[:, 2:3], 4.0, None, ALU.mult)
            dve.tensor_scalar(onehot[:], inv_f[:], expert_row[:, 0:1], None, ALU.is_equal).then_inc(prep_done, 1)

            def chunk_low(n):
                _, hi, lo, cols = chunks[n]
                dve.wait_ge(chunk_hi, n + 1)
                dve.tensor_tensor(lo, raw[n % NRAW][:, 0:cols], hi.bitcast(F32), ALU.subtract).then_inc(chunk_lo, 1)

            def mask_parts(g):
                p, c = divmod(g, 2)
                o = 64 * (p % 2)
                cols = slice(c * CHUNK, (c + 1) * CHUNK)
                dst = mask_w[:, p // 2, cols]
                dve.wait_ge(mask_full, g + 1)
                link(dve.tensor_tensor(mask_tmp[o:o + 48, 0:CHUNK], bank_y[0][o:o + 48, 0:CHUNK], pattern[o:o + 48, cols], ALU.mult))
                link(dve.tensor_copy(dst[o:o + 48], mask_tmp[o:o + 48, 0:CHUNK]))
                dve.tensor_tensor(dst[o + 32:o + 48], mask_tmp[o + 32:o + 48, 0:CHUNK], dst[o + 32:o + 48].bitcast(F32),
                                  ALU.subtract).then_inc(mask_done, 1)

            ln1(0, 0)
            dve.wait_ge(pmask_in, 16)
            for q in range(12):
                if q < 2 * PAIRS:
                    chunk_low(2 * q)
                    chunk_low(2 * q + 1)
                    mask_parts(q)
                elif q == 2 * PAIRS:
                    for n in range(4 * PAIRS, NCH):
                        chunk_low(n)
                for k in range((8 * q) // 3, (8 * q + 8) // 3):
                    dve_hook(k, 0)
            x2_low(0)
            top_k(0)
            soft_start(0)
            soft_end(0)
            for s in range(3):
                shared(0, s)
            st.end()
            st.start("turn", 1)
            experts(0, 1)
            with dve.Fori(2, NT) as T:
                st.start("turn", T)
                experts(T - 1, T)
                st.end()
            st.start("epilogue")
            experts(NT - 1, None)

        @block.scalar
        def _(act):
            st = Steps(act, act_step, "act")
            link = st.link

            def fn(out, src, f, **kw):
                return nc.scalar.activation(out, src, f, **kw)

            def a1(T, b):
                n = 2 * T + b
                wait(act, xt_full, n + 1)
                wait(act, out_full, n)
                fn(xt[:].rearrange("p k t -> p (k t)"), bank_a[:, :], ACT.Copy).then_inc(xt_ready, 1)

            def a2(T, b):
                n = 2 * T + b
                wait(act, xh_full, n + 1)
                wait(act, hr_ready, n)
                wait(act, hi_ready, n)
                for m in range(2):
                    fn(xh[:, m, :], bank_b[:, m * HALF:(m + 1) * HALF], ACT.Identity, bias=b_in[:, m:m + 1])\
                        .then_inc(xh_ready, 1)

            def a3(T, b):
                n = 2 * T + b
                wait(act, gates_full, n + 1)
                fn(tg[:], bank_a[:, 0:HALF], ACT.Tanh, bias=half_bg[:, 0:1], scale=0.5).then_inc(gates_read, 1)
                fn(gt[:, 0, :], bank_a[:, HALF:2 * HALF], ACT.Tanh, bias=half_bg[:, 1:2], scale=0.5)\
                    .then_inc(gates_read, 1)

            def a4(T, b):
                n = 2 * T + b
                wait(act, ga_ready, n + 1)
                fn(gt[:, 1, :], gt[:, 0, :], ACT.Tanh, scale=decay[:, 0:1]).then_inc(tanh_ready, 1)
                wait(act, ph_ready, n + 1)
                fn(sn[:], ph[:], ACT.Sin, scale=TWO_PI)
                link(fn(cs[:], ph[:], ACT.Abs))
                fn(cs[:], cs[:], ACT.Sin, scale=-TWO_PI, bias=consts[:, 1:2]).then_inc(trig_ready, 1)

            def a5(T, b):
                n = 2 * T + b
                wait(act, pq_ready, n + 1)
                fn(ph[:], gt[:], ACT.Square).then_inc(sq_ready, 1)
                wait(act, norm2_ready, n + 1)
                fn(w[1][:], w[0][:], ACT.Sqrt).then_inc(norm_ready, 1)
                wait(act, mp_ready, n + 1)
                fn(w[3][:], w[2][:], ACT.Sqrt, scale=0.5).then_inc(sr_ready, 1)

            def act_hook(slot, T):
                b, k = divmod(slot, 16)
                for at, stage in ((0, a1), (1, a2), (2, a3), (5, a4), (6, a5)):
                    if k == at:
                        stage(T, b)

            def x2_high(T):
                wait(act, up_full, 15 * T)
                for k, o in enumerate((bank_a, bank_b)):
                    wait(act, x2t_full, 2 * T + k + 1)
                    fn(x2_hi[:, k, :], o[:, :], ACT.Copy).then_inc(x2h_ready, 1)

            def router_exp(T):
                wait(act, rt_read, T + 1)
                fn(logit, logit, ACT.Exp).then_inc(exp_ready, 1)

            def chosen_copy(T):
                wait(act, ct_full, T + 1)
                wait(act, flat_full, T)
                fn(chosen_t, bank_b[:, 0:2 * P], ACT.Copy).then_inc(ct_ready, 1)

            def soft_exp_(T):
                wait(act, shifted, T + 1)
                fn(soft[:], soft[:], ACT.Exp).then_inc(soft_exp, 1)

            def stack_copy(T):
                for c, o in enumerate((bank_a, bank_b)):
                    wait(act, st_full, 2 * T + c + 1)
                    fn(stack[:, c, :], o[:, :], ACT.Copy).then_inc(st_copied, 1)

            def silu(N, m, j):
                wait(act, gate_full, N + 1)
                wait(act, hid_done, N - 2)
                fn(tmp[j][0:m, :], bank_g[0:m, :], ACT.Silu).then_inc(silu_done, 1)

            def wrep_copy(t, p):
                wait(act, wrep_full, 4 * t + p + 1)
                wait(act, lrd_done, 4 * t + max(p - 1, 0))
                if p == 0:
                    wait(act, yt_full, 2 * t)
                fn(wrep[p % 2][:], bank_r[:, :], ACT.Copy).then_inc(wrep_taken, 1)

            def y_copy(t):
                wait(act, pair_done, 4 * t + 4)
                for m in range(KH):
                    fn(y_sb[m][:], bank_y[m][:, :], ACT.Copy).then_inc(y_copied, 1)

            def res_copy(t):
                wait(act, stored, 32 * t)
                wait(act, xn2_ready, 2 * t + 2)
                fn(res[:].rearrange("p s d -> p (s d)"), x1[:].rearrange("p b s d -> p (b s d)"), ACT.Copy)\
                    .then_inc(res_copied, 1)

            def experts(t, T):
                wrep_copy(t, 0)
                for q in range(12):
                    p, j = divmod(q, 3)
                    hook = (lambda k: act_hook(8 * p + k, T)) if T is not None else (lambda k: None)
                    hook(2 * j)
                    silu(15 * t + 3 + q, WIDTH[j], j)
                    hook(2 * j + 1)
                    if j == 2:
                        if p < PAIRS - 1:
                            wrep_copy(t, p + 1)
                        hook(6)
                    if q == 1:
                        res_copy(t)
                if T is not None:
                    x2_high(T)
                    router_exp(T)
                    silu(15 * T, SW[0], 0)
                    y_copy(t)
                    chosen_copy(T)
                    silu(15 * T + 1, SW[1], 1)
                    soft_exp_(T)
                    silu(15 * T + 2, SW[2], 2)
                    stack_copy(T)
                else:
                    y_copy(t)

            st.start("prologue")
            act.wait_ge(prep_e, 1)
            link(fn(prep[:, 3:4], prep[:, 1:2], ACT.Exp))
            fn(prep[:, 3:4], prep[:, 3:4], ACT.Ln, bias=1.0).then_inc(prep_l, 1)
            act.wait_ge(small_in, 16 * 12)
            fn(select[:], lr_g[:, 0:3 * P + 2 * IR], ACT.Copy)
            act.wait_ge(prep_done, 1)

            def chunk_high(n):
                _, hi, _, cols = chunks[n]
                act.wait_ge(chunk_in[n % NRAW], 16 * (n // NRAW + 1))
                fn(hi, raw[n % NRAW][:, 0:cols], ACT.Copy).then_inc(chunk_hi, 1)

            for q in range(12):
                if q < 2 * PAIRS:
                    chunk_high(2 * q)
                    chunk_high(2 * q + 1)
                elif q == 2 * PAIRS:
                    for n in range(4 * PAIRS, NCH):
                        chunk_high(n)
                for k in range((8 * q) // 3, (8 * q + 8) // 3):
                    act_hook(k, 0)
            x2_high(0)
            router_exp(0)
            chosen_copy(0)
            soft_exp_(0)
            act.wait_ge(chunk_lo, NCH)
            for s in range(3):
                silu(s, SW[s], s)
            stack_copy(0)
            act.wait_ge(mask_done, 2 * PAIRS)
            act.wait_ge(scaled, 3)
            st.end()
            st.start("turn", 1)
            experts(0, 1)
            with act.Fori(2, NT) as T:
                st.start("turn", T)
                experts(T - 1, T)
                st.end()
            st.start("epilogue")
            experts(NT - 1, None)

        @block.gpsimd
        def _(pool):
            st = Steps(pool, pool_step, "pool")
            link = st.link

            def tt(out, a, b_, op):
                return nc.gpsimd.tensor_tensor(out, a, b_, op)

            def imag(T, b):
                n = 2 * T + b
                s, c = sn[:, 0, :], cs[:, 0, :]
                wait(pool, fac_ready, n + 1)
                link(tt(pw[0][:], gt[:, 0, :], s, ALU.mult))
                link(tt(pw[1][:], gt[:, 1, :], c, ALU.mult))
                tt(pw[2][:], pw[0][:], pw[1][:], ALU.add).then_inc(mi_ready, 1)
                wait(pool, mi_ready, n + 1)
                link(tt(pw[1][:], xh[:, 0, :], pw[2][:], ALU.mult))
                wait(pool, mr_ready, n + 1)
                link(tt(pw[0][:], xh[:, 1, :], w[2][:], ALU.mult))
                tt(pw[0][:], pw[0][:], pw[1][:], ALU.subtract).then_inc(bi_ready, 1)
                wait(pool, g_ready, n + 1)
                link(tt(pw[1][:], w[0][:], s, ALU.mult))
                link(tt(pw[2][:], w[1][:], c, ALU.mult))
                tt(xt[:, 1, :], pw[1][:], pw[2][:], ALU.add).then_inc(hi_ready, 1)

            def rstd(mv, rs, count, ready, signal, value):
                wait(pool, ready, value)
                link(tt(var_eps[:, 0:count], mv[:, 0:count, 1], powers[:, 0, 0:count], ALU.add))
                tt(rs[:, 0:count], var_eps[:, 0:count], powers[:, 1, 0:count], ALU.pow).then_inc(signal, 1)

            def turn_work(t, T):
                n = 2 * T
                if t is not None:
                    rstd(mv1, rs1, 2, var1, rs1_ready, n + 1)
                for b in range(B):
                    imag(T, b)
                    if b == 0:
                        rstd(mv1, rs1, 2, var1, rs1_ready, n + 2)
                    rstd(mv2, rs2, 2, var2, rs2_ready, n + b + 1)
                    rstd(mv3, rs3, 2, var3, rs3_ready, n + b + 1)
                if t is not None:
                    rstd(mv4, rs4, 4, var4, rs4_ready, t + 1)

            st.start("prologue")
            nc.gpsimd.memset(powers[:, 0, :], EPS)
            link(nc.gpsimd.memset(powers[:, 1, :], -0.5))
            rstd(mv1, rs1, 2, var1, rs1_ready, 1)
            for dst, name in ((qb, "w_qb"), (down, "w_down"), (dqa, "w_dqa"), (dqb, "w_dqb"), (sdown, "w_sdown")):
                d = dst[:, :, :, :] if len(dst.shape) == 4 else dst[:, :, :]
                pool.dma_start(d, A[name]).then_inc(wts_in, 16)

            def scales(r):
                for h in range(2):
                    src = A["s_qb"][:, 2 * r + h, :] if r < 2 else A["s_dqb"][:, 2 * H * h:2 * H * (h + 1)]
                    pool.dma_start(wrep[h][:, 0:src.shape[1]], src).then_inc(scale_in, 16)
                pool.wait_ge(wts_in, 16 * 5)
                pool.wait_ge(scale_in, 32 * (r + 1))
                for h in range(2):
                    o = qb[:, 2 * r + h, :] if r < 2 else \
                        dqb[:].rearrange("p a c -> p (a c)")[:, 2 * H * h:2 * H * (h + 1)]
                    last = tt(o, o, wrep[h][:, 0:o.shape[1]], ALU.mult)
                    link(last)
                pool.sem_inc(scaled, 1)

            scales(0)
            scales(1)
            scales(2)
            turn_work(None, 0)
            st.end()
            st.start("turn", 1)
            turn_work(0, 1)
            with pool.Fori(2, NT) as T:
                st.start("turn", T)
                turn_work(T - 1, T)
                st.end()
            st.start("epilogue")
            rstd(mv4, rs4, 4, var4, rs4_ready, NT)

        return found


INPUTS = [("x", (B, S, H)), ("w_gu", (P, PAIRS, KH, GU)), ("w_sgu", (P, KH, 2 * ISH)), ("w_router", (P, KH * E)),
          ("w_qb", (P, PAIRS, 2 * QUP)), ("s_qb", (P, PAIRS, 2 * QUP)), ("w_down", (P, PAIRS, 3, H)),
          ("w_dqa", (P, PAIRS, 5 * 64)), ("w_dqb", (P, PAIRS, H)), ("s_dqb", (P, PAIRS * H)), ("w_sdown", (P, 3, H)),
          ("mask_up", (P, KH * 2 * P)), ("w_in", (P, KH, H)), ("w_gate", (P, KH, H)), ("w_out", (P, KH, H)),
          ("b_in", (P, 2)), ("b_gate", (P, 2)), ("a_par", (P, 2)), ("b_out", (1, H)), ("inv", (P, E)),
          ("expert_row", (P, 1)), ("ident", (P, P)), ("select", (P, 3 * P + 2 * IR)), ("pattern", (P, GU))]


def lay_out(a):
    z = lambda *shape: np.zeros(shape, np.float32)
    rows = lambda m: m.reshape(KH, P, -1).transpose(1, 0, 2)

    gw, uw = a["L0_ffn_gate_W"], a["L0_ffn_up_W"]
    w_gu = z(P, PAIRS, KH, GU)
    w_qb, s_qb = z(P, PAIRS, 2 * QUP), z(P, PAIRS, 2 * QUP)
    w_down, w_dqa = z(P, PAIRS, 3, H), z(P, PAIRS, 5 * 64)
    w_dqb, s_dqb = z(P, PAIRS, H), z(P, PAIRS, H)
    for p in range(PAIRS):
        for up, (wt, qa, qbw, sc) in enumerate(((gw, "L0_ffn_gate_qa", "L0_ffn_gate_qb", "L0_ffn_gate_scale"),
                                                (uw, "L0_ffn_up_qa", "L0_ffn_up_qb", "L0_ffn_up_scale"))):
            for e in range(2):
                f = 2 * p + e
                wt_t, qa_t = rows(wt[f].T), rows(a[qa][f].reshape(K * R, H).T)
                q = a[qbw][f].transpose(0, 2, 1).reshape(K * R, I)
                scale = np.broadcast_to(a[sc][f], (K * R, I))
                r = slice(64 * e, 64 * e + 64)
                for c, d, i0, n in ((P * e, 0, 0, P), (2 * P + IR * e, P + IR * e, P, IR)):
                    c, d = c + up * UP0, d + up * QUP
                    w_gu[:, p, :, c:c + n] = wt_t[:, :, i0:i0 + n]
                    w_qb[r, p, d:d + n] = q[:, i0:i0 + n]
                    s_qb[r, p, d:d + n] = scale[:, i0:i0 + n]
                c = LR0 + up * P + 64 * e
                w_gu[:, p, :, c:c + 64] = qa_t
        for e in range(2):
            f = 2 * p + e
            dw = a["L0_ffn_down_W"][f].T
            qa = a["L0_ffn_down_qa"][f].reshape(K * R, I).T
            w_down[:, p, e, :] = dw[:P]
            w_down[IR * e:IR * (e + 1), p, 2, :] = dw[P:]
            w_dqa[:, p, 128 * e:128 * e + 64] = qa[:P]
            w_dqa[IR * e:IR * (e + 1), p, 192 + 64 * e:256 + 64 * e] = qa[P:]
            w_dqb[64 * e:64 * e + 64, p] = a["L0_ffn_down_qb"][f].transpose(0, 2, 1).reshape(K * R, H)
            s_dqb[64 * e:64 * e + 64, p] = np.broadcast_to(a["L0_ffn_down_scale"][f], (K * R, H))
    w_sgu = np.concatenate([rows(a["L0_ffn_sh_gate_W"].T), rows(a["L0_ffn_sh_up_W"].T)], axis=2)
    sd = np.concatenate([a["L0_ffn_sh_down_W"].T, z(3 * P - ISH, H)]).reshape(3, P, H).transpose(1, 0, 2)
    mask_up = z(P, KH, 2, P)
    for p in range(PAIRS):
        both = rows(a["L0_ffn_mask_up_W"][2 * p:2 * p + 2].transpose(1, 0, 2).reshape(H, 2 * K))
        for g in range(3):
            c = 64 * (p % 2) + 16 * g
            mask_up[:, :, p // 2, c:c + 16] = both
    w_gate = z(H, 2, P)
    n_in, n_out = a["L0_attn_W_gx"].shape[1:]
    for h in range(a["L0_attn_W_gx"].shape[0]):
        w_gate[n_in * h:n_in * (h + 1), 0, n_out * h:n_out * (h + 1)] = a["L0_attn_W_gx"][h]
        w_gate[n_in * h:n_in * (h + 1), 1, n_out * h:n_out * (h + 1)] = a["L0_attn_W_ga"][h]
    b_gate = np.stack([a["L0_attn_b_gx"].reshape(P), a["L0_attn_b_ga"].reshape(P)], axis=1)

    select, pattern = z(P, 3 * P + 2 * IR), z(P, GU)
    for o in (0, 64):
        for e in range(2):
            for k in range(K):
                c = 64 * e + 8 * k
                select[o + 8 * e + k, c:c + 8] = 1
                select[o + 16 + 8 * e + k, c:c + 8] = 1
            for r in (o + 48 + e, o + 50 + e):
                select[r, P + P * e:P + P * (e + 1)] = 1
                select[r, 3 * P + IR * e:3 * P + IR * (e + 1)] = 1
            for g in range(3):
                r = slice(o + 16 * g + 8 * e, o + 16 * g + 8 * e + 8)
                for up in range(2):
                    pattern[r, up * UP0 + P * e:up * UP0 + P * (e + 1)] = 1
                    pattern[r, up * UP0 + 2 * P + IR * e:up * UP0 + 2 * P + IR * (e + 1)] = 1
                    pattern[r, LR0 + up * P + 64 * e:LR0 + up * P + 64 * e + 64] = 1
    d = {"x": a["L0_attn_x"], "w_gu": w_gu, "w_sgu": w_sgu, "w_router": rows(a["L0_ffn_gate_weight"].T),
         "w_qb": w_qb, "s_qb": s_qb, "w_down": w_down, "w_dqa": w_dqa, "w_dqb": w_dqb, "s_dqb": s_dqb,
         "w_sdown": sd, "mask_up": mask_up, "w_in": rows(a["L0_attn_W_in"]), "w_gate": rows(w_gate.reshape(H, H)),
         "w_out": rows(a["L0_attn_W_out"]), "b_in": a["L0_attn_b_in"].reshape(2, P).T, "b_gate": b_gate,
         "a_par": np.stack([a["L0_attn_a_real"], a["L0_attn_a_imag"]], axis=1), "b_out": a["L0_attn_b_out"],
         "inv": np.broadcast_to(a["L0_ffn_inv_mapping"].reshape(1, E), (P, E)),
         "expert_row": np.arange(P, dtype=np.float32) % E, "ident": np.eye(P, dtype=np.float32),
         "select": select, "pattern": pattern}
    return {"in_" + n: np.ascontiguousarray(d[n]).reshape(shape) for n, shape in INPUTS}


def kernel(**inputs):
    import concourse.bacc as bacc
    from concourse.bass_utils import run_bass_kernel_spmd

    arrays = lay_out({n: np.asarray(v) for n, v in inputs.items()})
    steps = {}
    for _ in range(2):
        nc = bacc.Bacc("TRN2", target_bir_lowering=False, num_devices=1)
        aps = {n: nc.dram_tensor("in_" + n, shape, I32 if n == "inv" else F32, kind="ExternalInput").ap()
               for n, shape in INPUTS}
        aps["out"] = nc.dram_tensor("out", (B, S, H), F32, kind="ExternalOutput").ap()
        steps = build(nc, aps, steps)
    r = run_bass_kernel_spmd(nc, [arrays], core_ids=[0])
    return r.results[0]["out"]
```

```python
import math
from contextlib import ExitStack

import numpy as np
import concourse.bass as bass
from concourse import mybir

F32, F32R, F16, I32 = mybir.dt.float32, mybir.dt.float32r, mybir.dt.float16, mybir.dt.int32
ALU, ACT, AX = mybir.AluOpType, mybir.ActivationFunctionType, mybir.AxisListType

P = 128
B, S, H = 2, 2048, 256
KH = H // P
HALF = 256
TOK = B * HALF
NT = S // HALF
SUB = TOK // P
F, K, R, I = 8, 8, 8, 176
E = F * K
PAIRS = F // 2
IR = I - P
ISH = 2 * I
TOP = 6
WIDTH = [P, P, 2 * IR]
COL = [0, P, 2 * P]
GU = 2 * (2 * P + 2 * IR) + 2 * P
UP0 = 2 * P + 2 * IR
LR0 = 2 * UP0
CHUNK = GU // 2
QCOL = [0, 0, P]
QUP = P + 2 * IR
SW = [P, P, ISH - 2 * P]
EPS = 1e-5
ROUND1 = 1.5 * 2.0 ** 23
ROUND12 = 1.5 * 2.0 ** 11
TWO_PI = 6.2831850
TINY = 1e-30
OFF = -1e9
PE_AT = {"gates": (1, 21), "out": (18, 37), "t1": (None, 18), "xh": (0, 18), "x2_turn": (42,),
         "router": (46,), "chosen": (47,), "flat": (47,), "stack": (52,)}
DVE_AT = {"turns": (0, 13), "sums": (1, 14), "radius": (2, 15), "step": (3, 17), "modulus": (5, 18),
          "root": (6, 19), "input": (7, 21), "scan_re": (8, 21), "scan_im": (9, 22), "x_stats": (None, 9),
          "norm_in": (None, 9), "stats": (11, 24), "sum": (11, 25), "norm_out": (25,), "top_start": (30,),
          "top_end": (30,), "soft": (32,), "soft_end": (33,), "x2_low": (30,)}
ACT_AT = {"xt": (None, 11), "xh": (1, 12), "gates": (1, 13), "trig": (3, 16), "squares": (5, 19),
          "roots": (5, 19), "x2_copy": (28,), "exp": (30,), "chosen": (32,), "soft": (32,), "stack": (36,),
          "x2_high": (30,)}
LATE = (0, 1, 0, 0, 0, 4, 2, 1, 6, 8, 4)
MASKS = (0, 0, 0, 0, 2, 2, 2, 2, 2, 3, 8, 8, 8)
POOL_AT = {"input": (7, 19), "scan": (7, 21), "back": (8, 22)}
LOW = 2.0 ** 12


def build(nc, A, steps):
    ctx = ExitStack()
    with ctx:
        def sb(name, shape, dt=F32):
            return ctx.enter_context(nc.sbuf_tensor(name, shape, dt))

        def bank(name):
            return ctx.enter_context(nc.psum_tensor(name, [P, 512], F32))

        def sem(name):
            return ctx.enter_context(nc.semaphore(name))

        gu_hi, gu_lo = sb("gu_hi", [P, PAIRS, KH, GU], F32R), sb("gu_lo", [P, PAIRS, KH, GU], F16)
        sgu_hi, sgu_lo = sb("sgu_hi", [P, KH, 2 * ISH], F32R), sb("sgu_lo", [P, KH, 2 * ISH], F16)
        mask_w = sb("mask_w", [P, 2, GU], F32R)
        router = sb("router", [P, KH * E])
        select = sb("select", [P, 3 * P + 2 * IR], F32R)
        qb_hi, qb_lo = (sb(f"qb_{x}", [P, PAIRS, 2 * QUP], F32R) for x in ("hi", "lo"))
        down_hi, down_lo = (sb(f"down_{x}", [P, PAIRS, 3, H], F32R) for x in ("hi", "lo"))
        dqa_hi, dqa_lo = (sb(f"dqa_{x}", [P, PAIRS, 5 * 64], F32R) for x in ("hi", "lo"))
        sdown_hi, sdown_lo = (sb(f"sdown_{x}", [P, 3, H], F32R) for x in ("hi", "lo"))
        dqb = sb("dqb", [P, PAIRS, H])
        w_in, w_gate, w_out = sb("w_in", [P, KH, H]), sb("w_gate", [P, KH, 2, 64]), sb("w_out", [P, KH, H])
        ident, onehot = sb("ident", [P, P]), sb("onehot", [P, E])
        expert_row = sb("expert_row", [P, 1])
        b_in, b_gate, a_par = sb("b_in", [P, 2]), sb("b_gate", [P, 2]), sb("a_par", [P, 2])
        half_bg, decay, turns, prep = sb("half_bg", [P, 2]), sb("decay", [P, 1]), sb("turns", [P, 1]), sb("prep", [P, 4])
        half_pi = sb("half_pi", [P, 1])
        b_out = sb("b_out", [33, H], F32R)
        inv_i, inv_f = sb("inv_i", [P, E], I32), sb("inv_f", [P, E])
        row_ones = sb("row_ones", [33, P], F32R)
        ones = sb("ones", [P, 1])

        x_in = sb("x_in", [P, B, 2, H])
        x1 = sb("x1", [P, B, 2, H])
        res = sb("res", [P, SUB, H])
        xt = sb("xt", [P, 2, HALF])
        xh = sb("xh", [P, 2, HALF])
        tg = sb("tg", [P, HALF])
        gt = sb("gt", [P, 2, HALF])
        trig = sb("trig", [P, 3, 2, HALF])
        ph = trig[:, 0]
        sn, cs = trig[:, 1], trig[:, 2]
        w4 = sb("w4", [P, 4, HALF])
        w = [w4[:, i, :] for i in range(4)]
        rad = sb("rad", [P, HALF])
        pw3 = sb("pw3", [P, 3, HALF])
        pw = [pw3[:, i, :] for i in range(3)]
        xn = pw3[:, 0:2, :]
        xn2 = w4[:].rearrange("p (b s) d -> p b s d", b=B)
        carry = sb("carry", [P, B, 4])
        bn1, bn2, bn3, bn4 = (sb(f"bn{i}", [P, 4, 6]) for i in range(1, 5))
        mv1, mv2, mv3, mv4 = (sb(f"mv{i}", [P, 4, 2]) for i in range(1, 5))
        powers, var_eps = sb("powers", [P, 2, 4]), sb("var_eps", [P, 4, 4])
        rs1, rs2, rs3, rs4 = (sb(f"rs{i}", [P, 4]) for i in range(1, 5))
        nm4, spare, inv_low = sb("nm4", [P, 4]), sb("spare", [P, 1]), sb("inv_low", [P, 1])

        logit = w[0].rearrange("p (s e) -> p s e", e=E)
        soft, flat = w[1], w[2]
        chosen = w[3].rearrange("p (s e) -> p s e", e=E)
        x2_t = [xt[:].rearrange("p k t -> p (k t)"), xn.rearrange("p s d -> p (s d)")]
        chosen_t = pw3[:, 2, :]
        rmax, rsum, rinv = sb("rmax", [P, SUB]), sb("rsum", [P, SUB]), sb("rinv", [P, SUB])
        score = xh[:].rearrange("p k t -> p (k t)")[:, 0:SUB * (E + 2)].rearrange("p (s e) -> p s e", s=SUB)
        left = gt[:].rearrange("p k t -> p (k t)")[:, 0:SUB * (E + 2)].rearrange("p (s e) -> p s e", s=SUB)
        top8 = sb("top8", [P, SUB, 8])
        gmax, gsum, ginv, scal = (sb(n, [P, SUB * F]) for n in ("gmax", "gsum", "ginv", "scal"))
        stack_tm = trig[:, 0:2].rearrange("p a k t -> p (a k t)").rearrange("p (s a c) -> p s a c", a=PAIRS, c=64)

        x2_16 = sb("x2_16", [P, KH, TOK], F16)
        x2_hi, x2_lo = sb("x2_hi", [P, KH, TOK], F32R), sb("x2_lo", [P, KH, TOK], F32R)
        stack = sb("stack", [P, 2, TOK], F32R)
        tmp = [sb(f"tmp{i}", [P, TOK]) for i in range(2)]
        TMP = [0, 1, 0]
        hid_hi, hid_lo = ([sb(f"hid_{x}{i}", [P, TOK], F32R) for i in range(3)] for x in ("hi", "lo"))
        lrg_hi, lrg_lo, lru_hi, lru_lo = (sb(n, [P, TOK], F32R) for n in ("lrg_hi", "lrg_lo", "lru_hi", "lru_lo"))
        lr_d = sb("lr_d", [P, TOK])
        wrep = [sb(f"wrep{i}", [P, TOK]) for i in range(2)]
        y_sb = wrep

        bank_a, bank_b = bank("bank_a"), bank("bank_b")
        bank_r, bank_g, bank_u, bank_d = bank("bank_r"), bank("bank_g"), bank("bank_u"), bank("bank_d")
        bank_y = [bank("bank_y0"), bank("bank_y1")]
        mask_bank = bank_y + [bank_r, bank_d, bank_g, bank_u]

        S_ = {}
        def named(*names):
            for n in names:
                S_[n] = sem(n)
            return [S_[n] for n in names]
        small_in, pmask_in, dqb_in, ident_in, later_in, onehot_done = named(
            "small_in", "pmask_in", "dqb_in", "ident_in", "later_in", "onehot_done")
        chunk_in = named(*(f"chunk_in{i}" for i in range(6)))
        chunk_done = named(*(f"chunk_done{i}" for i in range(6)))
        chunk_hi, chunk_rest, chunk_scaled, mask_full, mask_done, prep_e, prep_l, prep_done = named(
            "chunk_hi", "chunk_rest", "chunk_scaled", "mask_full", "mask_done", "prep_e", "prep_l", "prep_done")
        x_loaded0, x_loaded1, x_used = named("x_loaded0", "x_loaded1", "x_used")
        x_loaded = [x_loaded0, x_loaded1]
        var1, rs1_ready, xn_ready, xt_full, xt_ready, xh_full, xh_ready = named(
            "var1", "rs1_ready", "xn_ready", "xt_full", "xt_ready", "xh_full", "xh_ready")
        gates_full, gates_read, ga_ready, tanh_ready, ph_ready, trig_ready = named(
            "gates_full", "gates_read", "ga_ready", "tanh_ready", "ph_ready", "trig_ready")
        pq_ready, sq_ready, norm2_ready, norm_ready, mp_ready, sr_ready, fac_ready = named(
            "pq_ready", "sq_ready", "norm2_ready", "norm_ready", "mp_ready", "sr_ready", "fac_ready")
        mr_ready, mi_ready, bi_ready, g_ready, hr_ready, hi_ready, out_full, out_read = named(
            "mr_ready", "mi_ready", "bi_ready", "g_ready", "hr_ready", "hi_ready", "out_full", "out_read")
        var2, rs2_ready, var3, rs3_ready, xn2_ready = named("var2", "rs2_ready", "var3", "rs3_ready", "xn2_ready")
        x2t_full, x2t_ready, x2h_ready, x2s_ready, x2l_ready, rt_full, rt_read, exp_ready, chosen_ready, ct_full, ct_ready = named(
            "x2t_full", "x2t_ready", "x2h_ready", "x2s_ready", "x2l_ready", "rt_full", "rt_read", "exp_ready", "chosen_ready", "ct_full",
            "ct_ready")
        flat_full, flat_read, shifted, soft_exp, stm_ready, st_full, st_copied = named(
            "flat_full", "flat_read", "shifted", "soft_exp", "stm_ready", "st_full", "st_copied")
        gate_full, up_full, silu_done, hid_done, srep_full, srep_taken, wrep_full, wrep_taken = named(
            "gate_full", "up_full", "silu_done", "hid_done", "srep_full", "srep_taken", "wrep_full", "wrep_taken")
        mask_added, lrg_full, lru_full, lrd_full, lrg_done, lru_done, lrd_done, sdown_used, pair_done = named(
            "mask_added", "lrg_full", "lru_full", "lrd_full", "lrg_done", "lru_done", "lrd_done", "sdown_used", "pair_done")
        y_copied, yt_full, var4, rs4_ready, nm4_ready, yt_read, final_ready, res_copied, stored = named(
            "y_copied", "yt_full", "var4", "rs4_ready", "nm4_ready", "yt_read", "final_ready", "res_copied", "stored")
        hid_high, hid_low, lrg_high, lrg_low, lru_high, lru_low = named(
            "hid_high", "hid_low", "lrg_high", "lrg_low", "lru_high", "lru_low")
        dve_step, act_step, pool_step = named("dve_step", "act_step", "pool_step")

        block = ctx.enter_context(nc.Block())

        def wait(eng, s, value):
            if not (isinstance(value, int) and value <= 0):
                eng.wait_ge(s, value)

        class Steps:
            def __init__(self, eng, s, name):
                self.eng, self.sem, self.name, self.base, self.k = eng, s, name, 0, 0
                self.seen = {}

            def link(self, ins):
                self.k += 1
                ins.then_inc(self.sem, 1)
                self.eng.wait_ge(self.sem, self.base + self.k)

            def start(self, part, i=None):
                n0, n1 = steps.get((self.name, "prologue"), 0), steps.get((self.name, "turn"), 0)
                self.base = {"prologue": 0, "turn": None if i is None else n0 + (i - 1) * n1,
                             "epilogue": n0 + (NT - 1) * n1}[part]
                self.k, self.part = 0, part

            def end(self):
                self.seen[(self.name, self.part)] = self.k
                found[(self.name, self.part)] = self.k

        found = {}

        xv = A["x"].rearrange("b (t s p) d -> b t p s d", p=P, s=2)
        ov = A["out"].rearrange("b (t s p) d -> b t p s d", p=P, s=2)

        gate_up, chunks = [], []
        for p in range(PAIRS):
            for c in range(2):
                for k in range(KH):
                    cols = slice(c * CHUNK, (c + 1) * CHUNK)
                    gate_up.append((A["w_gu"][:, p, k, cols], CHUNK, gu_hi[:, p, k, cols], gu_lo[:, p, k, cols], None))
        for k in range(KH):
            for c in range(2):
                cols = slice(c * ISH, (c + 1) * ISH)
                chunks.append((A["w_sgu"][:, k, cols], ISH, sgu_hi[:, k, cols], sgu_lo[:, k, cols], None))
        chunks.append((A["select"], 3 * P + 2 * IR, select[:, :], None, None))
        early = chunks[-1]

        def piece(src, hi, lo, rank):
            names = " ".join("abc"[:rank])
            flat = lambda v: v.rearrange(f"p {names} -> p ({names})")
            src, hi, lo = flat(src), flat(hi), flat(lo)
            n = src.shape[1]
            for c in range(0, n, 512):
                m = min(512, n - c)
                chunks.append((src[:, c:c + m], m, hi[:, c:c + m], lo[:, c:c + m], None))

        piece(A["w_sdown"], sdown_hi[:, :, :], sdown_lo[:, :, :], 2)
        for p in range(PAIRS):
            chunks.append((A["w_qb"][:, p, :], 2 * QUP, qb_hi[:, p, :], qb_lo[:, p, :], "next"))
            chunks.append((A["s_qb"][:, p, :], 2 * QUP, None, None, "scale"))
        piece(A["w_down"], down_hi[:, :, :, :], down_lo[:, :, :, :], 3)
        piece(A["w_dqa"], dqa_hi[:, :, :], dqa_lo[:, :, :], 2)
        for h in range(2):
            chunks.append((A["s_dqb"][:, 2 * H * h:2 * H * (h + 1)], 2 * H, None, None, h))
        others, chunks, masked, late = chunks, [], [], []
        for q in range(12):
            if q < 2 * PAIRS:
                masked.append(len(chunks))
                chunks += gate_up[KH * q:KH * (q + 1)]
            n = LATE[q] if q < 11 else len(others)
            late.append(range(len(chunks), len(chunks) + n))
            chunks, others = chunks + others[:n], others[n:]
        NCH = len(chunks)
        EARLY = 1 + [c is early for c in chunks].index(True)
        highs = [sum(c[3] is not None for c in chunks[:n + 1]) for n in range(NCH)]
        halves = [sum(c[3] is not None and c[3].dtype == F16 for c in chunks[:n + 1]) for n in range(NCH)]

        def wait_chunks(eng, n):
            for i in range(NRAW):
                eng.wait_ge(chunk_done[i], len(range(i, n, NRAW)))

        dqb_all = dqb[:].rearrange("p a c -> p (a c)")
        raw = [dqb_all[:, 0:2 * H], dqb_all[:, 2 * H:4 * H], tmp[0], tmp[1], wrep[0], wrep[1]]
        NRAW = len(raw)
        pattern = res[:, :, :].rearrange("p s d -> p (s d)")

        @block.sync
        def _(sp):
            sp.dma_start(x_in[:, 0], xv[0, 0]).then_inc(x_loaded[0], 16)
            sp.dma_start(ident[:, :], A["ident"]).then_inc(ident_in, 16)
            for dst, src in ((w_in, "w_in"), (lr_d, "mask_up"), (w_gate, "w_gate")):
                d = dst[tuple(slice(None) for _ in dst.shape)]
                sp.dma_start(d, A[src]).then_inc(small_in, 16)
            for n, (src, cols, *_) in enumerate(chunks):
                if n == KH:
                    sp.dma_start(pattern[:, 0:GU], A["pattern"]).then_inc(pmask_in, 16)
                    sp.dma_start(x_in[:, 1], xv[1, 0]).then_inc(x_loaded[1], 16)
                if n >= NRAW:
                    sp.wait_ge(chunk_done[n % NRAW], n // NRAW)
                sp.dma_start(raw[n % NRAW][:, 0:cols], src).then_inc(chunk_in[n % NRAW], 16)
                if n == NCH - 2:
                    for i in range(2):
                        sp.wait_ge(chunk_done[i], len(range(i, n, NRAW)))
                    sp.dma_start(dqb[:, :, :], A["w_dqb"]).then_inc(dqb_in, 16)

            def load(T):
                for b in range(B):
                    sp.wait_ge(x_used, 2 * T - 1 + b)
                    sp.dma_start(x_in[:, b], xv[b, T]).then_inc(x_loaded[b], 16)

            def store(t):
                sp.wait_ge(final_ready, t + 1)
                for b in range(B):
                    sp.dma_start(ov[b, t], res[:, 2 * b:2 * b + 2, :]).then_inc(stored, 16)

            load(1)
            with sp.Fori(2, NT) as T:
                load(T)
                store(T - 2)
            store(NT - 2)
            store(NT - 1)
            sp.wait_ge(stored, 32 * NT)

        @block.tensor
        def _(pe):
            def mm(out, lhs, rhs, start, stop):
                return nc.tensor.matmul(out, lhs, rhs, start=start, stop=stop, skip_group_check=True)

            def split3(out, hi, lo, rhs_hi, rhs_lo, start, stop=False):
                mm(out, hi, rhs_hi, start, False)
                mm(out, hi, rhs_lo, False, False)
                return mm(out, lo, rhs_hi, False, stop)

            def split3n(out, hi, lo, k, start, stop=False):
                mm(out, hi, x2_hi[:, k, :], start, False)
                mm(out, hi, x2_lo[:, k, :], False, False)
                return mm(out, lo, x2_16[:, k, :], False, stop)

            def turn(out, src):
                return nc.tensor.transpose(out, src, ident[:, :])

            def t1(T, b):
                n = 2 * T + b
                pe.wait_ge(xn_ready, n + 1)
                if b == 0:
                    wait(pe, st_copied, 2 * T)
                else:
                    pe.wait_ge(xh_ready, 2 * n)
                for k in range(KH):
                    for s in range(2):
                        last = turn(bank_b[:, k * HALF + s * P:k * HALF + (s + 1) * P], xn[:, s, k * P:(k + 1) * P])
                last.then_inc(xt_full, 1)

            def xh_mm(T, b):
                n = 2 * T + b
                pe.wait_ge(xt_ready, n + 1)
                for m in range(2):
                    for k in range(KH):
                        last = mm(bank_b[:, m * HALF:(m + 1) * HALF], w_in[:, k, m * P:(m + 1) * P], xt[:, k, :],
                                  k == 0, k == KH - 1)
                last.then_inc(xh_full, 1)

            def gates_mm(T, b):
                n = 2 * T + b
                pe.wait_ge(xh_ready, 2 * (n + 1))
                if b:
                    pe.wait_ge(out_read, n)
                for m in range(2):
                    for k in range(KH):
                        last = mm(bank_a[64 * k:64 * k + 64, m * HALF:(m + 1) * HALF], w_gate[:, k, m, :], xh[:, k, :],
                                  True, True)
                last.then_inc(gates_full, 1)

            def out_mm(T, b):
                n = 2 * T + b
                pe.wait_ge(gates_read, 2 * (n + 1))
                pe.wait_ge(hr_ready, n + 1)
                pe.wait_ge(hi_ready, n + 1)
                for s in range(2):
                    o = bank_a[:, s * H:(s + 1) * H]
                    mm(o, row_ones[:, :], b_out[:, :], True, False)
                    for k in range(KH):
                        last = mm(o, xt[:, k, s * P:(s + 1) * P], w_out[:, k, :], False, k == KH - 1)
                last.then_inc(out_full, 1)

            def pe_hook(q, part, T):
                at = 4 * q + part
                for name, stage in (("out", out_mm), ("t1", t1), ("xh", xh_mm), ("gates", gates_mm)):
                    for b in range(B):
                        if at == PE_AT[name][b]:
                            stage(T, b)
                for name, stage in (("x2_turn", x2_turn), ("router", router_mm), ("chosen", chosen_turn),
                                    ("flat", flat_mm), ("stack", stack_turn)):
                    if at == PE_AT[name][0]:
                        stage(T)

            def x2_turn(T):
                pe.wait_ge(xn2_ready, T + 1)
                pe.wait_ge(out_read, 2 * T + 2)
                pe.wait_ge(xh_ready, 4 * T + 4)
                for k, o in enumerate((bank_a, bank_b)):
                    for b in range(B):
                        for s in range(2):
                            last = turn(o[:, (2 * b + s) * P:(2 * b + s + 1) * P], xn2[:, b, s, k * P:(k + 1) * P])
                    last.then_inc(x2t_full, 1)

            def router_mm(T):
                pe.wait_ge(x2t_ready, 2 * T + 2)
                for s in range(SUB):
                    for k in range(KH):
                        last = mm(bank_a[:, s * E:(s + 1) * E], x2_t[k][:, s * P:(s + 1) * P],
                                  router[:, k * E:(k + 1) * E], k == 0, k == KH - 1)
                last.then_inc(rt_full, 1)

            def chosen_turn(T):
                pe.wait_ge(chosen_ready, T + 1)
                for g in range(SUB // 2):
                    last = turn(bank_b[:, g * P:(g + 1) * P], w[3][:, g * P:(g + 1) * P])
                last.then_inc(ct_full, 1)

            def flat_mm(T):
                pe.wait_ge(ct_ready, T + 1)
                pe.wait_ge(rt_read, T + 1)
                for s in range(SUB):
                    last = mm((bank_a, bank_b)[s % 2][:, (s // 2) * E:(s // 2 + 1) * E],
                              chosen_t[E * (s % 2):E * (s % 2 + 1), (s // 2) * P:(s // 2 + 1) * P],
                              onehot[E * (s % 2):E * (s % 2 + 1), :], True, True)
                last.then_inc(flat_full, 1)

            def y_turn(t):
                pe.wait_ge(y_copied, 2 * t + 2)
                for g, o in enumerate(bank_y):
                    for s in range(2):
                        for k in range(KH):
                            last = turn(o[:, s * H + k * P:s * H + (k + 1) * P],
                                        y_sb[k][:, (2 * g + s) * P:(2 * g + s + 1) * P])
                    last.then_inc(yt_full, 1)

            def stack_turn(T):
                pe.wait_ge(stm_ready, T + 1)
                pe.wait_ge(flat_read, 2 * T + 2)
                for c, o in enumerate((bank_a, bank_b)):
                    for s in range(SUB):
                        last = turn(o[:, s * P:(s + 1) * P],
                                    stack_tm[:, s, 2 * c:2 * c + 2, :].rearrange("p a c -> p (a c)"))
                    last.then_inc(st_full, 1)

            def shared_in(t, s, up):
                N = 15 * t + s
                if s == 0 and not up:
                    pe.wait_ge(x2h_ready, 2 * t + 2)
                    pe.wait_ge(x2l_ready, 2 * t + 2)
                    pe.wait_ge(x2s_ready, 2 * t + 2)
                m = SW[s]
                c = up * ISH + s * P
                o = (bank_u if up else bank_g)[0:m, :]
                wait(pe, hid_done if up else silu_done, N)
                for k in range(KH):
                    last = split3n(o, sgu_hi[:, k, c:c + m], sgu_lo[:, k, c:c + m], k, k == 0, k == KH - 1)
                last.then_inc(up_full if up else gate_full, 1)

            def shared_down(t, m):
                if m == 0:
                    pe.wait_ge(hid_low, 15 * t + 3)
                    wait(pe, yt_read, t)
                for j in range(3):
                    r, c = slice(0, SW[j]), slice(m * P, (m + 1) * P)
                    last = split3(bank_y[m][:, :], sdown_hi[r, j, c], sdown_lo[r, j, c], hid_hi[j][r, :],
                                  hid_lo[j][r, :], j == 0)
                last.then_inc(sdown_used, 1)

            def base(p):
                return 64 * (p % 2), p // 2

            def srep(t, q):
                p, j = divmod(q, 3)
                o, c = base(p)
                if j == 0:
                    pe.wait_ge(wrep_taken, 4 * t + p + 1)
                else:
                    pe.wait_ge(srep_taken, 12 * t + q)
                mm(bank_r[0:WIDTH[j], :], select[o:o + 64, P + COL[j]:P + COL[j] + WIDTH[j]], stack[o:o + 64, c, :],
                   True, True).then_inc(srep_full, 1)

            def in_mm(t, q, up):
                p, j = divmod(q, 3)
                o, c = base(p)
                N = 15 * t + 3 + q
                m = WIDTH[j]
                cols = slice(up * UP0 + COL[j], up * UP0 + COL[j] + m)
                out = (bank_u if up else bank_g)[0:m, :]
                if up:
                    pe.wait_ge(hid_done, N)
                elif j == 0:
                    pe.wait_ge(lru_done, 4 * t + p + 1)
                else:
                    pe.wait_ge(silu_done, N)
                mm(out, mask_w[o:o + 64, c, cols], stack[o:o + 64, c, :], True, False).then_inc(mask_added, 1)
                for k in range(KH):
                    split3n(out, gu_hi[:, p, k, cols], gu_lo[:, p, k, cols], k, False)
                pe.wait_ge(lru_low if up else lrg_low, 4 * t + p + 1)
                pe.wait_ge(mask_added, 24 * t + 2 * q + up + 1)
                rows = (slice(0, 64), slice(64, P), slice(0, P))[j]
                q0 = up * QUP + QCOL[j]
                qc = slice(q0, q0 + m)
                hi, lo = (lru_hi, lru_lo) if up else (lrg_hi, lrg_lo)
                split3(out, qb_hi[rows, p, qc], qb_lo[rows, p, qc], hi[rows, :], lo[rows, :], False, True)\
                    .then_inc(up_full if up else gate_full, 1)

            def low_rank_in(t, p):
                o, c = base(p)
                for up, (out, full) in enumerate(((bank_d, lrg_full), (bank_g, lru_full))):
                    if up:
                        pe.wait_ge(silu_done, 15 * t + 3 + 3 * p)
                    elif p == 1:
                        pe.wait_ge(lrg_done, 4 * t + 1)
                    else:
                        wait(pe, lrd_done, 4 * t + max(p - 1, 0))
                    cols = slice(LR0 + up * P, LR0 + (up + 1) * P)
                    for k in range(KH):
                        split3n(out[:, :], gu_hi[:, p, k, cols], gu_lo[:, p, k, cols], k, k == 0)
                    if p == 0 and not up:
                        pe.wait_ge(st_copied, 2 * t + 2)
                    mm(out[:, :], mask_w[o:o + 64, c, cols], stack[o:o + 64, c, :], False, True).then_inc(full, 1)
                    if not up:
                        wait(pe, srep_taken, 12 * t + 3 * p)
                        mm(bank_r[:, :], select[o:o + 64, 0:P], stack[o:o + 64, c, :], True, True)\
                            .then_inc(wrep_full, 1)

            def pair_down(t, p):
                for j in range(3):
                    pe.wait_ge(hid_low, 15 * t + 3 + 3 * p + j + 1)
                    r = slice(0, WIDTH[j])
                    for m in range(KH):
                        c = slice(m * P, (m + 1) * P)
                        split3(bank_y[m][:, :], down_hi[r, p, j, c], down_lo[r, p, j, c], hid_hi[j][r, :],
                               hid_lo[j][r, :], False)
                if p < PAIRS - 1:
                    pe.wait_ge(lrg_done, 4 * t + p + 2)
                else:
                    pe.wait_ge(lrd_done, 4 * t + p)
                for j, c in enumerate((0, 64, 192)):
                    r, c = slice(0, WIDTH[j]), slice(c, c + P)
                    last = split3(bank_d[:, :], dqa_hi[r, p, c], dqa_lo[r, p, c], hid_hi[j][r, :], hid_lo[j][r, :],
                                  j == 0, j == 2)
                last.then_inc(lrd_full, 1)

            def low_rank_out(t, p):
                pe.wait_ge(lrd_done, 4 * t + p + 1)
                for m in range(KH):
                    last = mm(bank_y[m][:, :], dqb[:, p, m * P:(m + 1) * P], lr_d[:, :], False, p == PAIRS - 1)
                last.then_inc(pair_done, 1)

            def experts(t, T):
                hook = (lambda q, part: pe_hook(q, part, T)) if T is not None else (lambda q, part: None)
                low_rank_in(t, 0)
                if T is not None:
                    t1(T, 0)
                for q in range(12):
                    p, j = divmod(q, 3)
                    hook(q, 0)
                    srep(t, q)
                    in_mm(t, q, 0)
                    if q == 0:
                        shared_down(t, 0)
                    hook(q, 1)
                    in_mm(t, q, 1)
                    if q == 0:
                        shared_down(t, 1)
                    hook(q, 2)
                    if j == 0 and p:
                        low_rank_out(t, p - 1)
                    if j == 2:
                        if p < PAIRS - 1:
                            low_rank_in(t, p + 1)
                        pair_down(t, p)
                        hook(q, 3)
                if T is None:
                    low_rank_out(t, PAIRS - 1)
                    y_turn(t)
                    return
                shared_in(T, 0, 0)
                hook(12, 0)
                shared_in(T, 0, 1)
                hook(12, 1)
                low_rank_out(t, PAIRS - 1)
                hook(12, 2)
                shared_in(T, 1, 0)
                shared_in(T, 1, 1)
                hook(12, 3)
                y_turn(t)
                shared_in(T, 2, 0)
                shared_in(T, 2, 1)
                hook(13, 0)

            pe.wait_ge(ident_in, 16)
            mask_l = lr_d[:, :].rearrange("p (k c m) -> p k c m", k=KH, c=2)

            def mask_mm(g):
                if g >= len(mask_bank):
                    pe.wait_ge(mask_done, g - len(mask_bank) + 1)
                for k in range(KH):
                    n = masked[g] + k
                    pe.wait_ge(chunk_in[n % NRAW], 16 * (n // NRAW + 1))
                    last = mm(mask_bank[g % len(mask_bank)][:, 0:CHUNK], mask_l[:, k, g // 4, :], raw[n % NRAW][:, 0:CHUNK], k == 0, k == 1)
                last.then_inc(mask_full, 1)

            t1(0, 0)
            pe.wait_ge(small_in, 16 * 6)
            for q in range(12):
                if q == 4:
                    pe.wait_ge(later_in, 16 * 6)
                    pe.wait_ge(onehot_done, 1)
                if q < 2 * PAIRS:
                    mask_mm(q)
                for part in range(4):
                    pe_hook(q, part, 0)
            wait_chunks(pe, EARLY)
            shared_in(0, 0, 0)
            pe_hook(12, 0, 0)
            shared_in(0, 0, 1)
            pe_hook(12, 1, 0)
            pe_hook(12, 2, 0)
            shared_in(0, 1, 0)
            shared_in(0, 1, 1)
            pe_hook(12, 3, 0)
            shared_in(0, 2, 0)
            shared_in(0, 2, 1)
            pe_hook(13, 0, 0)
            wait_chunks(pe, NCH)
            experts(0, 1)
            with pe.Fori(2, NT) as T:
                experts(T - 1, T)
            experts(NT - 1, None)

        @block.vector
        def _(dve):
            st = Steps(dve, dve_step, "dve")
            link = st.link

            def settle():
                dve.memset(spare[:], 0.0)

            def norm_stats(bn, mv, srcs, signal):
                for i, src in enumerate(srcs):
                    last = dve.bn_stats(bn[:, i, :], src)
                link(last)
                settle()
                for i in range(len(srcs)):
                    last = dve.bn_aggr(mv[:, i, :], bn[:, i, :])
                last.then_inc(signal, 1)


            def x_stats(T, b):
                dve.wait_ge(x_loaded[b], 16 * (T + 1))
                norm_stats(bn1, mv1, [x_in[:, b, s, :] for s in range(2)], var1)

            def ln1(T, b):
                n = 2 * T + b
                dve.wait_ge(rs1_ready, n + 1)
                wait(dve, hi_ready, n)
                for s in range(2):
                    last = dve.tensor_scalar(xn[:, s, :], x_in[:, b, s, :], mv1[:, s, 0:1], rs1[:, s:s + 1],
                                             ALU.subtract, ALU.mult)
                last.then_inc(xn_ready, 1)

            def e1a(T, b):
                n = 2 * T + b
                dve.wait_ge(gates_read, 2 * (n + 1))
                ga = gt[:, 0, :]
                dve.tensor_scalar(ga, ga, 0.5, 0.5, ALU.mult, ALU.add).then_inc(ga_ready, 1)
                dve.wait_ge(ga_ready, n + 1)
                link(dve.tensor_scalar(w[0], ga, turns[:, 0:1], None, ALU.mult))
                link(dve.tensor_scalar(w[1], w[0], ROUND1, ROUND1, ALU.add, ALU.subtract))
                link(dve.tensor_tensor(ph[:, 1, :], w[0], w[1], ALU.subtract))
                link(dve.tensor_scalar(w[0], ph[:, 1, :], ROUND12, ROUND12, ALU.add, ALU.subtract))
                link(dve.tensor_tensor(w[1], ph[:, 1, :], w[0], ALU.subtract))

            def e1b(T, b):
                dve.tensor_tensor_scan(w[2], ones[:].to_broadcast([P, HALF]), w[0], carry[:, b, 0:1], ALU.mult, ALU.add)
                link(dve.tensor_tensor_scan(w[3], ones[:].to_broadcast([P, HALF]), w[1], carry[:, b, 1:2], ALU.mult, ALU.add))
                link(dve.tensor_tensor(w[0], w[2], w[3], ALU.add))
                link(dve.tensor_scalar(w[1], w[0], ROUND1, ROUND1, ALU.add, ALU.subtract))
                link(dve.tensor_tensor(w[2], w[2], w[1], ALU.subtract))
                dve.tensor_copy(carry[:, b, 0:1], w[2][:, HALF - 1:HALF])
                dve.tensor_copy(carry[:, b, 1:2], w[3][:, HALF - 1:HALF])
                link(dve.tensor_tensor(ph[:, 0, :], w[2], w[3], ALU.add))
                dve.tensor_scalar(ph[:, 0, :], ph[:, 0, :], -0.5, 0.5, ALU.max, ALU.min).then_inc(ph_ready, 1)

            def e2a(T, b):
                n = 2 * T + b
                th = gt[:, 1, :]
                dve.wait_ge(tanh_ready, n + 1)
                link(dve.tensor_scalar(w[0], th, 1.0, None, ALU.add))
                link(dve.reciprocal(w[1], w[0]))
                dve.tensor_scalar(rad[:], w[1], 2.0, -1.0, ALU.mult, ALU.add)
                link(dve.scalar_tensor_tensor(out=w[0], in0=th, scalar=4.0, in1=w[1], op0=ALU.mult, op1=ALU.mult))
                link(dve.tensor_tensor(w[2], w[0], w[1], ALU.mult))

            def e2b(T, b):
                n = 2 * T + b
                dve.wait_ge(trig_ready, n + 1)
                dve.tensor_tensor(w[0], rad[:], sn[:, 1, :], ALU.mult)
                link(dve.tensor_tensor(w[1], rad[:], cs[:, 1, :], ALU.mult))
                link(dve.scalar_tensor_tensor(out=w[3], in0=w[0], scalar=2.0, in1=w[0], op0=ALU.mult, op1=ALU.mult))
                dve.scalar_tensor_tensor(out=gt[:, 1, :], in0=w[0], scalar=2.0, in1=w[1], op0=ALU.mult, op1=ALU.mult)
                dve.tensor_tensor(gt[:, 0, :], w[3], w[2], ALU.add).then_inc(pq_ready, 1)
                dve.tensor_scalar(tg[:], tg[:], 0.5, 0.5, ALU.mult, ALU.add)

            def e2c(T, b):
                n = 2 * T + b
                dve.wait_ge(sq_ready, n + 1)
                dve.tensor_tensor(w[0], ph[:, 0, :], ph[:, 1, :], ALU.add).then_inc(norm2_ready, 1)
                dve.wait_ge(norm_ready, n + 1)
                dve.tensor_tensor(w[2], w[1], gt[:, 0, :], ALU.add).then_inc(mp_ready, 1)

            def e3(T, b):
                n = 2 * T + b
                dve.wait_ge(sr_ready, n + 1)
                link(dve.tensor_scalar(w[0], w[3], 2.0, TINY, ALU.mult, ALU.max))
                link(dve.reciprocal(w[1], w[0]))
                link(dve.tensor_tensor(w[2], gt[:, 1, :], w[1], ALU.mult))
                dve.tensor_tensor(gt[:, 0, :], w[3], tg[:], ALU.mult)
                dve.tensor_tensor(gt[:, 1, :], w[2], tg[:], ALU.mult).then_inc(fac_ready, 1)

            def e4a(T, b):
                n = 2 * T + b
                dve.wait_ge(fac_ready, n + 1)
                s, c = sn[:, 0, :], cs[:, 0, :]
                dve.tensor_tensor(w[0], gt[:, 0, :], c, ALU.mult)
                link(dve.tensor_tensor(w[1], gt[:, 1, :], s, ALU.mult))
                dve.tensor_tensor(w[2], w[0], w[1], ALU.subtract).then_inc(mr_ready, 1)

            def e4b(T, b):
                n = 2 * T + b
                dve.wait_ge(mr_ready, n + 1)
                dve.tensor_tensor(w[0], xh[:, 0, :], w[2], ALU.mult)
                dve.wait_ge(mi_ready, n + 1)
                link(dve.tensor_tensor(w[1], xh[:, 1, :], pw[2], ALU.mult))
                link(dve.tensor_tensor(w[3], w[0], w[1], ALU.add))
                link(dve.tensor_tensor_scan(w[0], rad[:], w[3], carry[:, b, 2:3], ALU.mult, ALU.add))

            def e4c(T, b):
                n = 2 * T + b
                s, c = sn[:, 0, :], cs[:, 0, :]
                dve.wait_ge(bi_ready, n + 1)
                dve.tensor_tensor_scan(w[1], rad[:], pw[0], carry[:, b, 3:4], ALU.mult, ALU.add)\
                   .then_inc(g_ready, 1)
                dve.wait_ge(g_ready, n + 1)
                dve.tensor_copy(carry[:, b, 2:3], w[0][:, HALF - 1:HALF])
                dve.tensor_copy(carry[:, b, 3:4], w[1][:, HALF - 1:HALF])
                dve.tensor_tensor(w[2], w[0], c, ALU.mult)
                link(dve.tensor_tensor(w[3], w[1], s, ALU.mult))
                dve.tensor_tensor(xt[:, 0, :], w[2], w[3], ALU.subtract).then_inc(hr_ready, 1)

            def e6a(T, b):
                n = 2 * T + b
                dve.wait_ge(out_full, n + 1)
                norm_stats(bn2, mv2, [bank_a[:, s * H:(s + 1) * H] for s in range(2)], var2)

            def e6b(T, b):
                n = 2 * T + b
                dve.wait_ge(rs2_ready, n + 1)
                wait(dve, res_copied, T)
                for s in range(2):
                    last = dve.tensor_scalar(x1[:, b, s, :], bank_a[:, s * H:(s + 1) * H], mv2[:, s, 0:1],
                                             rs2[:, s:s + 1], ALU.subtract, ALU.mult)
                last.then_inc(out_read, 1)
                dve.wait_ge(out_read, n + 1)
                dve.tensor_tensor(x1[:, b], x1[:, b], x_in[:, b], ALU.add).then_inc(x_used, 1)
                dve.wait_ge(x_used, n + 1)
                norm_stats(bn3, mv3[:, 2 * b:2 * b + 2], [x1[:, b, s, :] for s in range(2)], var3)

            def e6c(T):
                dve.wait_ge(rs3_ready, 2 * T + 2)
                for b in range(B):
                    for s in range(2):
                        last = dve.tensor_scalar(xn2[:, b, s, :], x1[:, b, s, :], mv3[:, 2 * b + s, 0:1],
                                                 rs3[:, 2 * b + s:2 * b + s + 1], ALU.subtract, ALU.mult)
                last.then_inc(xn2_ready, 1)

            def dve_hook(slot, T):
                for name, stage in (("turns", e1a), ("sums", e1b), ("radius", e2a), ("step", e2b), ("modulus", e2c), ("root", e3),
                                    ("input", e4a), ("scan_re", e4b), ("scan_im", e4c), ("x_stats", x_stats), ("norm_in", ln1),
                                    ("stats", e6a), ("sum", e6b)):
                    for b in range(B):
                        if slot == DVE_AT[name][b]:
                            stage(T, b)
                for name, stage in (("norm_out", e6c), ("top_start", top_k_start), ("top_end", top_k_end), ("x2_low", x2_low),
                                    ("soft", soft_start), ("soft_end", soft_end)):
                    if slot == DVE_AT[name][0]:
                        stage(T)

            def x2_low(T):
                wait(dve, up_full, 15 * T)
                for k in range(KH):
                    dve.wait_ge(x2h_ready, 2 * T + k + 1)
                    dve.tensor_tensor(x2_lo[:, k, :], x2_t[k], x2_hi[:, k, :].bitcast(F32), ALU.subtract)\
                       .then_inc(x2l_ready, 1)

            def top_k_start(T):
                dve.wait_ge(rt_full, T + 1)
                lg = bank_a[:, 0:SUB * E].rearrange("p (s e) -> p s e", e=E)
                link(dve.tensor_reduce(rmax[:], lg, AX.X, ALU.max))
                dve.tensor_tensor(logit, lg, rmax[:].unsqueeze(2).to_broadcast([P, SUB, E]), ALU.subtract)\
                   .then_inc(rt_read, 1)

            def top_k_end(T):
                dve.wait_ge(exp_ready, T + 1)
                link(dve.tensor_reduce(rsum[:], logit, AX.X, ALU.add))
                link(dve.reciprocal(rinv[:], rsum[:]))
                dve.memset(score[:, :, E:E + 2], 2.0)
                link(dve.tensor_tensor(score[:, :, 0:E], logit, rinv[:].unsqueeze(2).to_broadcast([P, SUB, E]), ALU.mult))
                settle()
                for s in range(SUB):
                    last = dve.max(top8[:, s, :], score[:, s, :])
                link(last)
                settle()
                for s in range(SUB):
                    last = dve.match_replace(left[:, s, :], top8[:, s, :], score[:, s, :], 0.0)
                link(last)
                dve.tensor_tensor(chosen, score[:, :, 0:E], left[:, :, 0:E], ALU.subtract).then_inc(chosen_ready, 1)

            def soft_start(T):
                dve.wait_ge(flat_full, T + 1)
                for h, o in enumerate((bank_a, bank_b)):
                    dve.tensor_copy(flat[:].rearrange("p (g h e) -> p g h e", h=2, e=E)[:, :, h, :],
                                    o[:, 0:2 * E].rearrange("p (g e) -> p g e", e=E)).then_inc(flat_read, 1)
                dve.wait_ge(flat_read, 2 * T + 2)
                fg = flat[:].rearrange("p (g k) -> p g k", k=K)
                sg = soft[:].rearrange("p (g k) -> p g k", k=K)
                dve.tensor_reduce(scal[:], fg, AX.X, ALU.add)
                link(dve.tensor_scalar(soft[:], flat[:], 0.0, OFF, ALU.is_equal, ALU.mult))
                link(dve.tensor_tensor(soft[:], soft[:], flat[:], ALU.add))
                link(dve.tensor_reduce(gmax[:], sg, AX.X, ALU.max))
                dve.tensor_tensor(sg, sg, gmax[:].unsqueeze(2).to_broadcast([P, SUB * F, K]), ALU.subtract)\
                   .then_inc(shifted, 1)

            def soft_end(T):
                sg = soft[:].rearrange("p (g k) -> p g k", k=K)
                dve.wait_ge(soft_exp, T + 1)
                link(dve.tensor_reduce(gsum[:], sg, AX.X, ALU.add))
                link(dve.reciprocal(ginv[:], gsum[:]))
                link(dve.tensor_tensor(sg, sg, ginv[:].unsqueeze(2).to_broadcast([P, SUB * F, K]), ALU.mult))
                dve.memset(stack_tm[:, :, :, 52:64], 0.0)
                st_v = stack_tm.rearrange("p s a c -> p (s a) c")
                sv = soft[:].rearrange("p (g k) -> p g k", k=2 * K)
                cv = scal[:].rearrange("p (g k) -> p g k", k=2)
                dve.tensor_copy(st_v[:, :, 48:50].bitcast(F32R), cv)
                dve.tensor_copy(st_v[:, :, 32:48].bitcast(F32R), sv)
                link(dve.tensor_copy(st_v[:, :, 0:16].bitcast(F32R), sv))
                dve.tensor_tensor(st_v[:, :, 50:52], cv, st_v[:, :, 48:50], ALU.subtract)
                dve.tensor_tensor(st_v[:, :, 16:32], sv, st_v[:, :, 0:16], ALU.subtract).then_inc(stm_ready, 1)

            def y_halves():
                return [bank_y[s // 2][:, (s % 2) * H:(s % 2 + 1) * H] for s in range(SUB)]

            def y_stats(t):
                dve.wait_ge(yt_full, 2 * t + 2)
                norm_stats(bn4, mv4, y_halves(), var4)

            def y_norm(t):
                dve.wait_ge(rs4_ready, t + 1)
                dve.wait_ge(res_copied, t + 1)
                dve.scalar_tensor_tensor(out=nm4[:], in0=mv4[:, :, 0], scalar=-1.0, in1=rs4[:], op0=ALU.mult,
                                         op1=ALU.mult).then_inc(nm4_ready, 1)
                for s, y in enumerate(y_halves()):
                    last = dve.scalar_tensor_tensor(out=res[:, s, :], in0=y, scalar=rs4[:, s:s + 1],
                                                    in1=res[:, s, :], op0=ALU.mult, op1=ALU.add)
                last.then_inc(yt_read, 1)

            def y_shift(t):
                dve.wait_ge(yt_read, t + 1)
                dve.wait_ge(nm4_ready, t + 1)
                for s in range(SUB):
                    last = dve.tensor_scalar(res[:, s, :], res[:, s, :], nm4[:, s:s + 1], None, ALU.add)
                last.then_inc(final_ready, 1)

            def hidden(t, N, m, j, scaled_by, between=None):
                dve.wait_ge(silu_done, N + 1)
                if scaled_by is not None:
                    dve.wait_ge(srep_full, scaled_by + 1)
                    dve.tensor_tensor(tmp[TMP[j]][0:m, :], tmp[TMP[j]][0:m, :], bank_r[0:m, :], ALU.mult).then_inc(srep_taken, 1)
                    if between:
                        between()
                    dve.wait_ge(srep_taken, scaled_by + 1)
                dve.wait_ge(up_full, N + 1)
                dve.tensor_tensor(tmp[TMP[j]][0:m, :], tmp[TMP[j]][0:m, :], bank_u[0:m, :], ALU.mult).then_inc(hid_done, 1)

            def shared(t, s):
                hidden(t, 15 * t + s, SW[s], s, None)

            def low_rank(t, p):
                dve.wait_ge(wrep_taken, 4 * t + p + 1)
                dve.wait_ge(lrg_full, 4 * t + p + 1)
                dve.wait_ge(hid_low, 15 * t + 3 + 3 * p - 1)
                dve.tensor_tensor(tmp[1][:], bank_d[:, :], wrep[p % 2][:], ALU.mult).then_inc(lrg_done, 1)
                dve.wait_ge(lru_full, 4 * t + p + 1)
                dve.wait_ge(hid_low, 15 * t + 3 + 3 * p)
                dve.tensor_tensor(tmp[0][:], bank_g[:, :], wrep[p % 2][:], ALU.mult).then_inc(lru_done, 1)

            def low_rank_down(t, p):
                dve.wait_ge(lrd_full, 4 * t + p + 1)
                wait(dve, pair_done, 4 * t + p)
                dve.tensor_tensor(lr_d[:], bank_d[:, :], wrep[p % 2][:], ALU.mult).then_inc(lrd_done, 1)

            def experts(t, T, first=False):
                if T is not None:
                    x_stats(T, 0)
                if not first:
                    y_norm(t - 1)
                if T is not None:
                    ln1(T, 0)
                low_rank(t, 0)
                if not first:
                    y_shift(t - 1)
                for q in range(12):
                    p, j = divmod(q, 3)
                    hook = (lambda k: dve_hook(8 * p + k, T)) if T is not None else (lambda k: None)
                    hidden(t, 15 * t + 3 + q, WIDTH[j], j, 12 * t + q, lambda: hook(2 * j))
                    hook(2 * j + 1)
                    if j == 2:
                        if p < PAIRS - 1:
                            low_rank(t, p + 1)
                        hook(6)
                        low_rank_down(t, p)
                        hook(7)
                if T is not None:
                    dve_hook(32, T)
                    shared(T, 0)
                    dve_hook(33, T)
                    shared(T, 1)
                    dve_hook(34, T)
                    y_stats(t)
                    shared(T, 2)
                    dve_hook(35, T)
                else:
                    y_stats(t)
                    y_norm(t)
                    y_shift(t)

            st.start("prologue")
            dve.memset(carry[:], 0.0)
            dve.memset(ones[:], 1.0)
            dve.memset(row_ones[:].bitcast(F32), 1.0)
            dve.memset(b_out[:].bitcast(F32), 0.0)
            dve.memset(mask_w[:].bitcast(F32), 0.0)
            link(dve.memset(half_pi[:], math.pi / 2))
            x_stats(0, 0)
            ln1(0, 0)
            dve.wait_ge(small_in, 16 * 6)
            link(dve.tensor_scalar(prep[:, 0:1], a_par[:, 0:1], -1.0, None, ALU.mult))
            dve.tensor_tensor(prep[:, 1:2], prep[:, 0:1], a_par[:, 0:1], ALU.min).then_inc(prep_e, 1)
            dve.tensor_scalar(prep[:, 2:3], a_par[:, 0:1], 0.0, None, ALU.max)
            dve.tensor_scalar(turns[:], a_par[:, 1:2], 1.0 / (2 * math.pi), None, ALU.mult)
            link(dve.tensor_scalar(half_bg[:], b_gate[:], 0.5, None, ALU.mult))
            dve.wait_ge(prep_l, 1)
            link(dve.tensor_tensor(prep[:, 2:3], prep[:, 2:3], prep[:, 3:4], ALU.add))
            dve.tensor_scalar(decay[:], prep[:, 2:3], 4.0, None, ALU.mult).then_inc(prep_done, 1)

            def chunk_scale(n):
                _, cols, _, _, scale = chunks[n]
                if scale in (None, "scale"):
                    return
                m = n + 1 if scale == "next" else n
                s_m = raw[m % NRAW][:, 0:cols]
                dve.wait_ge(chunk_in[m % NRAW], 16 * (m // NRAW + 1))
                if scale == "next":
                    r = raw[n % NRAW][:, 0:cols]
                    dve.wait_ge(chunk_in[n % NRAW], 16 * (n // NRAW + 1))
                    k = sum(c[4] == "next" for c in chunks[:n + 1])
                    dve.tensor_tensor(r, r, s_m, ALU.mult).then_inc(chunk_scaled, 1)
                    dve.wait_ge(chunk_scaled, k)
                    dve.memset(spare[:], 0.0).then_inc(chunk_done[m % NRAW], 1)
                else:
                    dve.wait_ge(dqb_in, 16)
                    o = dqb[:].rearrange("p a c -> p (a c)")[:, 2 * H * scale:2 * H * (scale + 1)]
                    dve.tensor_tensor(o, o, s_m, ALU.mult).then_inc(chunk_done[m % NRAW], 1)

            def mask_parts(g):
                p, c = divmod(g, 2)
                o = 64 * (p % 2)
                cols = slice(c * CHUNK, (c + 1) * CHUNK)
                dst = mask_w[:, p // 2, cols]
                low = dst[o + 32:o + 48]
                dve.wait_ge(pmask_in, 16)
                dve.wait_ge(mask_full, g + 1)
                link(dve.tensor_tensor(dst[o:o + 48], mask_bank[g % len(mask_bank)][o:o + 48, 0:CHUNK], pattern[o:o + 48, cols], ALU.mult))
                link(dve.tensor_tensor(low, mask_bank[g % len(mask_bank)][o + 32:o + 48, 0:CHUNK], low.bitcast(F32), ALU.subtract))
                dve.tensor_tensor(low, low.bitcast(F32), pattern[o + 32:o + 48, cols], ALU.mult).then_inc(mask_done, 1)

            for q in range(12):
                if q == 3:
                    dve.wait_ge(later_in, 16 * 6)
                    dve.tensor_copy(b_out[0:1, :], x1[0:1, 0, 0, :])
                    dve.tensor_copy(b_out[32:33, :], x1[32:33, 0, 0, :])
                    link(dve.tensor_copy(inv_f[:], inv_i[:]))
                    dve.tensor_tensor(b_out[32:33, :], x1[32:33, 0, 0, :], b_out[32:33, :].bitcast(F32), ALU.subtract)
                    dve.tensor_scalar(onehot[:], inv_f[:], expert_row[:, 0:1], None, ALU.is_equal).then_inc(onehot_done, 1)
                for k in range((8 * q) // 3, (8 * q + 8) // 3):
                    dve_hook(k, 0)
                for g in range(MASKS[q], MASKS[q + 1]):
                    mask_parts(g)
                for n in late[q]:
                    chunk_scale(n)
            dve_hook(32, 0)
            shared(0, 0)
            dve_hook(33, 0)
            shared(0, 1)
            dve_hook(34, 0)
            shared(0, 2)
            dve_hook(35, 0)
            st.end()
            st.start("turn", 1)
            experts(0, 1, first=True)
            with dve.Fori(2, NT) as T:
                st.start("turn", T)
                experts(T - 1, T)
                st.end()
            st.start("epilogue")
            experts(NT - 1, None)

        @block.scalar
        def _(act):
            st = Steps(act, act_step, "act")
            link = st.link

            def fn(out, src, f, **kw):
                return nc.scalar.activation(out, src, f, **kw)

            def a1(T, b):
                n = 2 * T + b
                act.wait_ge(xt_full, n + 1)
                wait(act, out_full, n)
                fn(xt[:].rearrange("p k t -> p (k t)"), bank_b[:, :], ACT.Copy).then_inc(xt_ready, 1)

            def a2(T, b):
                n = 2 * T + b
                act.wait_ge(xh_full, n + 1)
                wait(act, hr_ready, n)
                wait(act, hi_ready, n)
                for m in range(2):
                    fn(xh[:, m, :], bank_b[:, m * HALF:(m + 1) * HALF], ACT.Identity, bias=b_in[:, m:m + 1])\
                        .then_inc(xh_ready, 1)

            def a3(T, b):
                n = 2 * T + b
                act.wait_ge(gates_full, n + 1)
                fn(tg[:], bank_a[:, 0:HALF], ACT.Tanh, bias=half_bg[:, 0:1], scale=0.5).then_inc(gates_read, 1)
                fn(gt[:, 0, :], bank_a[:, HALF:2 * HALF], ACT.Tanh, bias=half_bg[:, 1:2], scale=0.5)\
                    .then_inc(gates_read, 1)

            def a4(T, b):
                n = 2 * T + b
                act.wait_ge(ga_ready, n + 1)
                fn(gt[:, 1, :], gt[:, 0, :], ACT.Tanh, scale=decay[:, 0:1]).then_inc(tanh_ready, 1)
                act.wait_ge(ph_ready, n + 1)
                fn(sn, ph, ACT.Sin, scale=TWO_PI)
                link(fn(cs, ph, ACT.Abs))
                fn(cs, cs, ACT.Sin, scale=-TWO_PI, bias=half_pi[:]).then_inc(trig_ready, 1)

            def a5(T, b):
                n = 2 * T + b
                act.wait_ge(pq_ready, n + 1)
                fn(ph, gt[:], ACT.Square).then_inc(sq_ready, 1)

            def a6(T, b):
                n = 2 * T + b
                act.wait_ge(norm2_ready, n + 1)
                fn(w[1], w[0], ACT.Sqrt).then_inc(norm_ready, 1)
                act.wait_ge(mp_ready, n + 1)
                fn(w[3], w[2], ACT.Sqrt, scale=0.5).then_inc(sr_ready, 1)

            def act_hook(slot, T):
                for name, stage in (("xt", a1), ("xh", a2), ("gates", a3), ("trig", a4), ("squares", a5), ("roots", a6)):
                    for b in range(B):
                        if slot == ACT_AT[name][b]:
                            stage(T, b)
                for name, stage in (("x2_copy", x2_copy), ("exp", router_exp), ("x2_high", x2_high), ("chosen", chosen_copy),
                                    ("soft", soft_exp_), ("stack", stack_copy)):
                    if slot == ACT_AT[name][0]:
                        stage(T)

            def x2_copy(T):
                for k, o in enumerate((bank_a, bank_b)):
                    act.wait_ge(x2t_full, 2 * T + k + 1)
                    fn(x2_t[k], o[:, :], ACT.Copy).then_inc(x2t_ready, 1)

            def x2_high(T):
                wait(act, up_full, 15 * T)
                for k in range(KH):
                    act.wait_ge(x2t_ready, 2 * T + k + 1)
                    fn(x2_hi[:, k, :], x2_t[k], ACT.Copy).then_inc(x2h_ready, 1)

            def router_exp(T):
                act.wait_ge(rt_read, T + 1)
                fn(logit, logit, ACT.Exp).then_inc(exp_ready, 1)

            def chosen_copy(T):
                act.wait_ge(ct_full, T + 1)
                wait(act, flat_full, T)
                fn(chosen_t, bank_b[:, 0:2 * P], ACT.Copy).then_inc(ct_ready, 1)

            def soft_exp_(T):
                act.wait_ge(shifted, T + 1)
                fn(soft[:], soft[:], ACT.Exp).then_inc(soft_exp, 1)

            def stack_copy(T):
                for c, o in enumerate((bank_a, bank_b)):
                    act.wait_ge(st_full, 2 * T + c + 1)
                    fn(stack[:, c, :], o[:, :], ACT.Copy).then_inc(st_copied, 1)

            def silu(N, m, j, free, value):
                act.wait_ge(gate_full, N + 1)
                wait(act, free, value)
                fn(tmp[TMP[j]][0:m, :], bank_g[0:m, :], ACT.Silu).then_inc(silu_done, 1)

            def hid_parts(N, m, j, used, value):
                act.wait_ge(hid_done, N + 1)
                wait(act, used, value)
                fn(hid_hi[j][0:m, :], tmp[TMP[j]][0:m, :], ACT.Copy).then_inc(hid_high, 1)

            def shared(t, s):
                N = 15 * t + s
                silu(N, SW[s], s, hid_low, 15 * t + (1 if s == 2 else 0))
                hid_parts(N, SW[s], s, lrd_full, 4 * t)

            def low_rank_parts(t, p):
                act.wait_ge(up_full, 15 * t + 3 + 3 * p)
                act.wait_ge(lrg_done, 4 * t + p + 1)
                fn(lrg_hi[:], tmp[1][:], ACT.Copy).then_inc(lrg_high, 1)
                act.wait_ge(lru_done, 4 * t + p + 1)
                fn(lru_hi[:], tmp[0][:], ACT.Copy).then_inc(lru_high, 1)

            def wrep_copy(t, p):
                act.wait_ge(wrep_full, 4 * t + p + 1)
                wait(act, lrd_done, 4 * t + max(p - 1, 0))
                if p == 0:
                    wait(act, yt_full, 2 * t)
                fn(wrep[p % 2][:], bank_r[:, :], ACT.Copy).then_inc(wrep_taken, 1)

            def y_copy(t):
                act.wait_ge(pair_done, 4 * t + 4)
                for m in range(KH):
                    fn(y_sb[m][:], bank_y[m][:, :], ACT.Copy).then_inc(y_copied, 1)

            def res_copy(t):
                wait(act, stored, 32 * t)
                act.wait_ge(xn2_ready, t + 1)
                fn(res[:].rearrange("p s d -> p (s d)"), x1[:].rearrange("p b s d -> p (b s d)"), ACT.Copy)\
                    .then_inc(res_copied, 1)

            def experts(t, T):
                wrep_copy(t, 0)
                if T is not None:
                    a1(T, 0)
                low_rank_parts(t, 0)
                for q in range(12):
                    p, j = divmod(q, 3)
                    N = 15 * t + 3 + q
                    hook = (lambda k: act_hook(8 * p + k, T)) if T is not None else (lambda k: None)
                    hook(2 * j)
                    silu(N, WIDTH[j], j, (lru_low, lrg_low, hid_low)[j], 4 * t + p + 1 if j < 2 else N - 1)
                    hook(2 * j + 1)
                    hid_parts(N, WIDTH[j], j, *((lrd_full, 4 * t + p) if p else (sdown_used, KH * (t + 1))))
                    if j == 2:
                        if p < PAIRS - 1:
                            wrep_copy(t, p + 1)
                            low_rank_parts(t, p + 1)
                        hook(6)
                    if q == 1:
                        res_copy(t)
                if T is not None:
                    act_hook(32, T)
                    shared(T, 0)
                    act_hook(33, T)
                    y_copy(t)
                    act_hook(34, T)
                    shared(T, 1)
                    act_hook(35, T)
                    shared(T, 2)
                    act_hook(36, T)
                else:
                    y_copy(t)

            st.start("prologue")
            for dst, src in ((a_par, "a_par"), (b_gate, "b_gate"), (b_in, "b_in")):
                d = dst[tuple(slice(None) for _ in dst.shape)]
                act.dma_start(d, A[src]).then_inc(small_in, 16)
            for dst, src in ((inv_i, "inv"), (expert_row, "expert_row"), (w_out, "w_out"), (router, "w_router")):
                d = dst[tuple(slice(None) for _ in dst.shape)]
                act.dma_start(d, A[src]).then_inc(later_in, 16)
            for row in (0, 32):
                act.dma_start(x1[row:row + 1, 0, 0, :], A["b_out"]).then_inc(later_in, 16)
            act.wait_ge(prep_e, 1)
            link(fn(prep[:, 3:4], prep[:, 1:2], ACT.Exp))
            fn(prep[:, 3:4], prep[:, 3:4], ACT.Ln, bias=1.0).then_inc(prep_l, 1)
            a1(0, 0)
            act.wait_ge(small_in, 16 * 6)
            act.wait_ge(prep_done, 1)

            def chunk_high(n):
                for m in (n - 2, n) if n >= 2 else (n,):
                    _, cols, hi, lo, scale = chunks[m]
                    r = raw[m % NRAW][:, 0:cols]
                    if m < n and lo is not None and lo.dtype == F16:
                        act.wait_ge(chunk_rest, halves[m])
                        fn(lo, r, ACT.Copy, scale=LOW).then_inc(chunk_done[m % NRAW], 1)
                    if m == n and hi is not None:
                        if scale == "next":
                            act.wait_ge(chunk_scaled, sum(c[4] == "next" for c in chunks[:n + 1]))
                        else:
                            act.wait_ge(chunk_in[n % NRAW], 16 * (n // NRAW + 1))
                        fn(hi, r, ACT.Copy).then_inc(chunk_done[n % NRAW] if lo is None else chunk_hi, 1)

            for q in range(12):
                if q < 2 * PAIRS:
                    for k in range(KH):
                        chunk_high(masked[q] + k)
                for k in range((8 * q) // 3, (8 * q + 8) // 3):
                    act_hook(k, 0)
                for n in late[q]:
                    chunk_high(n)
            act_hook(32, 0)
            wait_chunks(act, NCH)
            shared(0, 0)
            act_hook(33, 0)
            act_hook(34, 0)
            shared(0, 1)
            act_hook(35, 0)
            shared(0, 2)
            act_hook(36, 0)
            act.wait_ge(mask_done, 2 * PAIRS)
            st.end()
            st.start("turn", 1)
            experts(0, 1)
            with act.Fori(2, NT) as T:
                st.start("turn", T)
                experts(T - 1, T)
                st.end()
            st.start("epilogue")
            experts(NT - 1, None)

        @block.gpsimd
        def _(pool):
            st = Steps(pool, pool_step, "pool")
            link = st.link

            def tt(out, a, b_, op):
                return nc.gpsimd.tensor_tensor(out, a, b_, op)

            def imag_a(T, b):
                n = 2 * T + b
                s, c = sn[:, 0, :], cs[:, 0, :]
                pool.wait_ge(fac_ready, n + 1)
                link(tt(pw[0], gt[:, 0, :], s, ALU.mult))
                link(tt(pw[1], gt[:, 1, :], c, ALU.mult))
                tt(pw[2], pw[0], pw[1], ALU.add).then_inc(mi_ready, 1)

            def imag_b(T, b):
                n = 2 * T + b
                pool.wait_ge(mi_ready, n + 1)
                link(tt(pw[1], xh[:, 0, :], pw[2], ALU.mult))
                pool.wait_ge(mr_ready, n + 1)
                link(tt(pw[0], xh[:, 1, :], w[2], ALU.mult))
                tt(pw[0], pw[0], pw[1], ALU.subtract).then_inc(bi_ready, 1)

            def imag_c(T, b):
                n = 2 * T + b
                s, c = sn[:, 0, :], cs[:, 0, :]
                pool.wait_ge(g_ready, n + 1)
                link(tt(pw[1], w[0], s, ALU.mult))
                link(tt(pw[2], w[1], c, ALU.mult))
                tt(xt[:, 1, :], pw[1], pw[2], ALU.add).then_inc(hi_ready, 1)

            def rstd(i, mv, rs, first, count, ready, signal, value):
                pool.wait_ge(ready, value)
                link(tt(var_eps[:, i, 0:count], mv[:, first:first + count, 1], powers[:, 0, 0:count], ALU.add))
                tt(rs[:, first:first + count], var_eps[:, i, 0:count], powers[:, 1, 0:count], ALU.pow).then_inc(signal, 1)

            def low(out, value, high, high_ready, n, signal):
                pool.wait_ge(high_ready, n + 1)
                tt(out, value, high.bitcast(F32), ALU.subtract).then_inc(signal, 1)

            def hid_rest(N, m, j):
                low(hid_lo[j][0:m, :], tmp[TMP[j]][0:m, :], hid_hi[j][0:m, :], hid_high, N, hid_low)

            def low_rank_rest(t, p):
                low(lrg_lo[:], tmp[1][:], lrg_hi[:], lrg_high, 4 * t + p, lrg_low)
                low(lru_lo[:], tmp[0][:], lru_hi[:], lru_high, 4 * t + p, lru_low)

            def x2_scaled(T):
                wait(pool, up_full, 15 * T)
                for k in range(KH):
                    pool.wait_ge(x2h_ready, 2 * T + k + 1)
                    tt(x2_16[:, k, :], x2_hi[:, k, :].bitcast(F32), inv_low[:].to_broadcast([P, TOK]), ALU.mult)\
                        .then_inc(x2s_ready, 1)

            def pool_hook(slot, T):
                for name, stage in (("input", imag_a), ("scan", imag_b), ("back", imag_c)):
                    for b in range(B):
                        if slot == POOL_AT[name][b]:
                            stage(T, b)
                for b in range(B):
                    n = 2 * T + b
                    if slot == DVE_AT["x_stats"][b]:
                        rstd(0, mv1, rs1, 0, 2, var1, rs1_ready, n + 1)
                    if slot == DVE_AT["stats"][b]:
                        rstd(1, mv2, rs2, 0, 2, var2, rs2_ready, n + 1)
                    if slot == DVE_AT["sum"][b]:
                        rstd(2, mv3, rs3, 2 * b, 2, var3, rs3_ready, n + 1)

            def experts(t, T):
                if T is not None:
                    rstd(0, mv1, rs1, 0, 2, var1, rs1_ready, 2 * T + 1)
                low_rank_rest(t, 0)
                for q in range(12):
                    p, j = divmod(q, 3)
                    hook = (lambda k: pool_hook(8 * p + k, T)) if T is not None else (lambda k: None)
                    hook(2 * j)
                    hid_rest(15 * t + 3 + q, WIDTH[j], j)
                    hook(2 * j + 1)
                    if j == 2:
                        if p < PAIRS - 1:
                            low_rank_rest(t, p + 1)
                        hook(6)
                        hook(7)
                if T is not None:
                    x2_scaled(T)
                    for s in range(3):
                        if s == 2:
                            rstd(3, mv4, rs4, 0, 4, var4, rs4_ready, t + 1)
                        hid_rest(15 * T + s, SW[s], s)
                else:
                    rstd(3, mv4, rs4, 0, 4, var4, rs4_ready, t + 1)

            st.start("prologue")
            nc.gpsimd.memset(powers[:, 0, :], EPS)
            nc.gpsimd.memset(inv_low[:], 1 / LOW)
            link(nc.gpsimd.memset(powers[:, 1, :], -0.5))
            rstd(0, mv1, rs1, 0, 2, var1, rs1_ready, 1)

            def chunk_low(n):
                _, cols, hi, lo, _ = chunks[n]
                r = raw[n % NRAW][:, 0:cols]
                if lo is None:
                    return
                if any(n in range(m, m + KH) for m in masked):
                    pool.wait_ge(mask_full, 1 + [n in range(m, m + KH) for m in masked].index(True))
                pool.wait_ge(chunk_hi, highs[n])
                if lo.dtype == F16:
                    tt(r, r, hi.bitcast(F32), ALU.subtract).then_inc(chunk_rest, 1)
                else:
                    tt(lo, r, hi.bitcast(F32), ALU.subtract).then_inc(chunk_done[n % NRAW], 1)

            for q in range(12):
                if q < 2 * PAIRS:
                    for k in range(KH):
                        chunk_low(masked[q] + k)
                for k in range((8 * q) // 3, (8 * q + 8) // 3):
                    pool_hook(k, 0)
                for n in late[q]:
                    chunk_low(n)
            x2_scaled(0)
            for s in range(3):
                hid_rest(s, SW[s], s)
            st.end()
            st.start("turn", 1)
            experts(0, 1)
            with pool.Fori(2, NT) as T:
                st.start("turn", T)
                experts(T - 1, T)
                st.end()
            st.start("epilogue")
            experts(NT - 1, None)

        return found


INPUTS = [("x", (B, S, H)), ("w_gu", (P, PAIRS, KH, GU)), ("w_sgu", (P, KH, 2 * ISH)), ("w_router", (P, KH * E)),
          ("w_qb", (P, PAIRS, 2 * QUP)), ("s_qb", (P, PAIRS, 2 * QUP)), ("w_down", (P, PAIRS, 3, H)),
          ("w_dqa", (P, PAIRS, 5 * 64)), ("w_dqb", (P, PAIRS, H)), ("s_dqb", (P, PAIRS * H)), ("w_sdown", (P, 3, H)),
          ("mask_up", (P, KH * 2 * P)), ("w_in", (P, KH, H)), ("w_gate", (P, KH, 2, 64)), ("w_out", (P, KH, H)),
          ("b_in", (P, 2)), ("b_gate", (P, 2)), ("a_par", (P, 2)), ("b_out", (1, H)), ("inv", (P, E)),
          ("expert_row", (P, 1)), ("ident", (P, P)), ("select", (P, 3 * P + 2 * IR)), ("pattern", (P, GU))]


def lay_out(a):
    z = lambda *shape: np.zeros(shape, np.float32)
    rows = lambda m: m.reshape(KH, P, -1).transpose(1, 0, 2)

    gw, uw = a["L0_ffn_gate_W"], a["L0_ffn_up_W"]
    w_gu = z(P, PAIRS, KH, GU)
    w_qb, s_qb = z(P, PAIRS, 2 * QUP), z(P, PAIRS, 2 * QUP)
    w_down, w_dqa = z(P, PAIRS, 3, H), z(P, PAIRS, 5 * 64)
    w_dqb, s_dqb = z(P, PAIRS, H), z(P, PAIRS, H)
    for p in range(PAIRS):
        for up, (wt, qa, qbw, sc) in enumerate(((gw, "L0_ffn_gate_qa", "L0_ffn_gate_qb", "L0_ffn_gate_scale"),
                                                (uw, "L0_ffn_up_qa", "L0_ffn_up_qb", "L0_ffn_up_scale"))):
            for e in range(2):
                f = 2 * p + e
                wt_t, qa_t = rows(wt[f].T), rows(a[qa][f].reshape(K * R, H).T)
                q = a[qbw][f].transpose(0, 2, 1).reshape(K * R, I)
                scale = np.broadcast_to(a[sc][f], (K * R, I))
                r = slice(64 * e, 64 * e + 64)
                for c, d, i0, n in ((P * e, 0, 0, P), (2 * P + IR * e, P + IR * e, P, IR)):
                    c, d = c + up * UP0, d + up * QUP
                    w_gu[:, p, :, c:c + n] = wt_t[:, :, i0:i0 + n]
                    w_qb[r, p, d:d + n] = q[:, i0:i0 + n]
                    s_qb[r, p, d:d + n] = scale[:, i0:i0 + n]
                c = LR0 + up * P + 64 * e
                w_gu[:, p, :, c:c + 64] = qa_t
        for e in range(2):
            f = 2 * p + e
            dw = a["L0_ffn_down_W"][f].T
            qa = a["L0_ffn_down_qa"][f].reshape(K * R, I).T
            w_down[:, p, e, :] = dw[:P]
            w_down[IR * e:IR * (e + 1), p, 2, :] = dw[P:]
            w_dqa[:, p, 128 * e:128 * e + 64] = qa[:P]
            w_dqa[IR * e:IR * (e + 1), p, 192 + 64 * e:256 + 64 * e] = qa[P:]
            w_dqb[64 * e:64 * e + 64, p] = a["L0_ffn_down_qb"][f].transpose(0, 2, 1).reshape(K * R, H)
            s_dqb[64 * e:64 * e + 64, p] = np.broadcast_to(a["L0_ffn_down_scale"][f], (K * R, H))
    w_sgu = np.concatenate([rows(a["L0_ffn_sh_gate_W"].T), rows(a["L0_ffn_sh_up_W"].T)], axis=2)
    sd = np.concatenate([a["L0_ffn_sh_down_W"].T, z(3 * P - ISH, H)]).reshape(3, P, H).transpose(1, 0, 2)
    mask_up = z(P, KH, 2, P)
    for p in range(PAIRS):
        both = rows(a["L0_ffn_mask_up_W"][2 * p:2 * p + 2].transpose(1, 0, 2).reshape(H, 2 * K))
        for g in range(3):
            c = 64 * (p % 2) + 16 * g
            mask_up[:, :, p // 2, c:c + 16] = both
    w_gate = z(H, 2, 64)
    n_in, n_out = a["L0_attn_W_gx"].shape[1:]
    for h in range(a["L0_attn_W_gx"].shape[0]):
        for g, name in enumerate(("L0_attn_W_gx", "L0_attn_W_ga")):
            w_gate[n_in * h:n_in * (h + 1), g, (n_out * h) % 64:(n_out * h) % 64 + n_out] = a[name][h]
    b_gate = np.stack([a["L0_attn_b_gx"].reshape(P), a["L0_attn_b_ga"].reshape(P)], axis=1)

    select, pattern = z(P, 3 * P + 2 * IR), z(P, GU)
    for o in (0, 64):
        for e in range(2):
            for k in range(K):
                c = 64 * e + 8 * k
                select[o + 8 * e + k, c:c + 8] = 1
                select[o + 16 + 8 * e + k, c:c + 8] = 1
            for r in (o + 48 + e, o + 50 + e):
                select[r, P + P * e:P + P * (e + 1)] = 1
                select[r, 3 * P + IR * e:3 * P + IR * (e + 1)] = 1
            for g in range(3):
                r = slice(o + 16 * g + 8 * e, o + 16 * g + 8 * e + 8)
                for up in range(2):
                    pattern[r, up * UP0 + P * e:up * UP0 + P * (e + 1)] = 1
                    pattern[r, up * UP0 + 2 * P + IR * e:up * UP0 + 2 * P + IR * (e + 1)] = 1
                    pattern[r, LR0 + up * P + 64 * e:LR0 + up * P + 64 * e + 64] = 1
    d = {"x": a["L0_attn_x"], "w_gu": w_gu, "w_sgu": w_sgu, "w_router": rows(a["L0_ffn_gate_weight"].T),
         "w_qb": w_qb, "s_qb": s_qb, "w_down": w_down, "w_dqa": w_dqa, "w_dqb": w_dqb, "s_dqb": s_dqb,
         "w_sdown": sd, "mask_up": mask_up, "w_in": rows(a["L0_attn_W_in"]), "w_gate": rows(w_gate.reshape(H, 2 * 64)).reshape(P, KH, 2, 64),
         "w_out": rows(a["L0_attn_W_out"]), "b_in": a["L0_attn_b_in"].reshape(2, P).T, "b_gate": b_gate,
         "a_par": np.stack([a["L0_attn_a_real"], a["L0_attn_a_imag"]], axis=1), "b_out": a["L0_attn_b_out"],
         "inv": np.broadcast_to(a["L0_ffn_inv_mapping"].reshape(1, E), (P, E)),
         "expert_row": np.arange(P, dtype=np.float32) % E, "ident": np.eye(P, dtype=np.float32),
         "select": select, "pattern": pattern}
    return {"in_" + n: np.ascontiguousarray(d[n]).reshape(shape) for n, shape in INPUTS}


def kernel(**inputs):
    import concourse.bacc as bacc
    from concourse.bass_utils import run_bass_kernel_spmd

    arrays = lay_out({n: np.asarray(v) for n, v in inputs.items()})
    steps = {}
    for _ in range(2):
        nc = bacc.Bacc("TRN2", target_bir_lowering=False, num_devices=1)
        aps = {n: nc.dram_tensor("in_" + n, shape, I32 if n == "inv" else F32, kind="ExternalInput").ap()
               for n, shape in INPUTS}
        aps["out"] = nc.dram_tensor("out", (B, S, H), F32, kind="ExternalOutput").ap()
        steps = build(nc, aps, steps)
    r = run_bass_kernel_spmd(nc, [arrays], core_ids=[0])
    return r.results[0]["out"]
```
